# Optimizing a Trainium2 kernel written in Bass

```python
import numpy as np
import jax
import jax.numpy as jnp

def _softmax(x, axis=-1):
    return jax.nn.softmax(x, axis=axis)

def _gelu(x):
    return jax.nn.gelu(x, approximate=True)

def _silu(x):
    return jax.nn.silu(x)

def _sigmoid(x):
    return jax.nn.sigmoid(x)

def _layernorm(x, axis=-1, eps=1e-05):
    m = jnp.mean(x, axis=axis, keepdims=True)
    v = jnp.var(x, axis=axis, keepdims=True)
    return (x - m) / jnp.sqrt(v + eps)

def _scatter_add(tgt, idx, src, axis=0):
    return tgt.at[idx].add(src)

def _segment_sum(src, seg, n):
    return jax.ops.segment_sum(src, seg, n)
kernel_name = 'mk_cond_seq_d4_seqx_r2_c45719'

def setup_inputs(seed: int=0):
    np.random.seed(seed)
    _w = jnp.asarray

    def _rec_inputs():
        import jax
        import jax.numpy as jnp
        _rk = jax.random.key(seed)
        x = -0.000125 + 0.9999 * jax.random.normal(jax.random.fold_in(_rk, 1), (8, 512, 512), jnp.float32)
        _lenS = 512 - jax.random.randint(jax.random.fold_in(_rk, 7), (8,), 0, max(1, 512 // 4) + 1, jnp.int32)
        _lenS2 = 512 - jax.random.randint(jax.random.fold_in(_rk, 8), (8,), 0, max(1, 512 // 4) + 1, jnp.int32)
        itok_B_0_15 = jax.random.randint(jax.random.fold_in(_rk, 11), (8,), 0, 16, jnp.int32)
        itok_B_34_63 = jax.random.randint(jax.random.fold_in(_rk, 13), (8,), 34, 64, jnp.int32)
        fside_Bx16xSxS_0 = -1.47943e-05 + 1.00017 * jax.random.normal(jax.random.fold_in(_rk, 14), (8, 16, 512, 512), jnp.float32)
        itok_B_0_7 = jax.random.randint(jax.random.fold_in(_rk, 15), (8,), 0, 8, jnp.int32)
        condB_dt = jax.random.uniform(jax.random.fold_in(_rk, 16), (8,), jnp.float32, 0.0, 0.981965)
        _validS = jnp.arange(512)[None, :] < _lenS[:, None]
        _validS2 = jnp.arange(512)[None, :] < _lenS2[:, None]
        _causal = jnp.tril(jnp.ones((512, 512), dtype=bool))
        mask_Bx1xSxS_bk0 = jnp.logical_not(jnp.broadcast_to(_validS[:, None, None, :], (8, 1, 512, 512)))
        return (x, itok_B_0_15, itok_B_34_63, fside_Bx16xSxS_0, itok_B_0_7, condB_dt, mask_Bx1xSxS_bk0)
    x, itok_B_0_15, itok_B_34_63, fside_Bx16xSxS_0, itok_B_0_7, condB_dt, mask_Bx1xSxS_bk0 = _rec_inputs()

    def _L0_cond_setup():
        import jax, jax.numpy as jnp
        import numpy as np
        B, S, D = (32, 512, 512)
        A = 128
        E = 16
        LN_EPS = 1e-05
        key = jax.random.key(seed)
        ks = jax.random.split(key, 10)
        s = lambda fan_in: 1.0 / np.sqrt(fan_in)
        return {'hidden_states': jax.random.normal(ks[0], (B, S, D), dtype=jnp.float32), 'domain_id': jax.random.randint(ks[1], (B,), 0, E, dtype=jnp.int64), 'down_W': jax.random.uniform(ks[2], (A, D), jnp.float32, -s(D), s(D)), 'down_b': jax.random.uniform(ks[3], (A,), jnp.float32, -s(D), s(D)), 'up_W': jax.random.uniform(ks[4], (D, A), jnp.float32, -s(A), s(A)), 'up_b': jax.random.uniform(ks[5], (D,), jnp.float32, -s(A), s(A)), 'expert_W': jax.random.uniform(ks[6], (E, A, A), jnp.float32, -s(A), s(A)), 'expert_b': jax.random.uniform(ks[7], (E, A), jnp.float32, -s(A), s(A)), 'domain_emb': jax.random.normal(ks[8], (E, A), dtype=jnp.float32), 'ln_gamma': jnp.ones((D,), jnp.float32), 'ln_beta': jnp.zeros((D,), jnp.float32)}
    _L0_cond_all = _L0_cond_setup()
    _L0_cond_in = {k: v for k, v in _L0_cond_all.items() if k in ('down_W', 'down_b', 'up_W', 'up_b', 'expert_W', 'expert_b', 'domain_emb', 'ln_gamma', 'ln_beta')}
    del _L0_cond_all

    def _L1_cond_setup():
        import jax, jax.numpy as jnp
        import numpy as np
        import math
        D_MODEL = 512
        N_HEAD = 16
        HEAD_DIM = D_MODEL // N_HEAD
        D_FF = 2048
        NUM_STEPS = 100.0
        RESCALE = 4000.0
        EPS = 1e-05

        def _sin_emb(t):
            half = D_MODEL // 2
            x = t.astype(jnp.float32) / NUM_STEPS * RESCALE
            freqs = jnp.exp(jnp.arange(half, dtype=jnp.float32) * (-math.log(10000.0) / (half - 1)))
            e = x[:, None] * freqs[None, :]
            return jnp.concatenate([jnp.sin(e), jnp.cos(e)], axis=-1)

        def _ln(x):
            m = jnp.mean(x, axis=-1, keepdims=True)
            v = jnp.var(x, axis=-1, keepdims=True)
            return (x - m) / jnp.sqrt(v + EPS)

        def _gelu2(x):
            return x * jax.nn.sigmoid(1.702 * x)
        key = jax.random.key(seed)
        ks = jax.random.split(key, 24)
        B, S, D, F = (4, 256, D_MODEL, D_FF)
        std = 0.02
        inp = {'src': jax.random.normal(ks[0], (B, S, D), dtype=jnp.float32), 'src_mask': jax.random.randint(ks[1], (B, 1, S, S), 0, 2).astype(bool), 'timestep': jax.random.randint(ks[2], (B,), 0, 100, dtype=jnp.int32), 'attention_bias': jax.random.normal(ks[3], (B, N_HEAD, S, S), dtype=jnp.float32), 'W_ada': jax.random.normal(ks[4], (D, 2 * D), dtype=jnp.float32) * std, 'b_ada': jnp.zeros((2 * D,), dtype=jnp.float32), 'Wq': jax.random.normal(ks[5], (D, D), dtype=jnp.float32) * std, 'bq': jnp.zeros((D,), dtype=jnp.float32), 'Wk': jax.random.normal(ks[6], (D, D), dtype=jnp.float32) * std, 'bk': jnp.zeros((D,), dtype=jnp.float32), 'Wv': jax.random.normal(ks[7], (D, D), dtype=jnp.float32) * std, 'bv': jnp.zeros((D,), dtype=jnp.float32), 'Wo': jax.random.normal(ks[8], (D, D), dtype=jnp.float32) * std, 'bo': jnp.zeros((D,), dtype=jnp.float32), 'W1': jax.random.normal(ks[9], (D, F), dtype=jnp.float32) * std, 'b1': jnp.zeros((F,), dtype=jnp.float32), 'W2': jax.random.normal(ks[10], (F, D), dtype=jnp.float32) * std, 'b2': jnp.zeros((D,), dtype=jnp.float32), 'g2': jnp.ones((D,), dtype=jnp.float32), 'beta2': jnp.zeros((D,), dtype=jnp.float32)}
        return inp
    _L1_cond_all = _L1_cond_setup()
    _L1_cond_in = {k: v for k, v in _L1_cond_all.items() if k in ('W_ada', 'b_ada', 'Wq', 'bq', 'Wk', 'bk', 'Wv', 'bv', 'Wo', 'bo', 'W1', 'b1', 'W2', 'b2', 'g2', 'beta2')}
    del _L1_cond_all

    def _L2_cond_setup():
        import jax, jax.numpy as jnp
        import numpy as np
        E, H, I = (8, 512, 2048)
        B, S = (4, 512)
        LN_EPS = 1e-12
        key = jax.random.key(seed)
        ks = jax.random.split(key, 8)
        x = jax.random.normal(ks[0], (B, S, H), dtype=jnp.float32)
        expert_idx = jax.random.randint(ks[1], (B,), 0, E, dtype=jnp.int64)
        Wi = jax.random.normal(ks[2], (E, H, I), dtype=jnp.float32) * 0.02
        bi = jnp.zeros((E, I), dtype=jnp.float32)
        Wo = jax.random.normal(ks[3], (E, I, H), dtype=jnp.float32) * 0.02
        bo = jnp.zeros((E, H), dtype=jnp.float32)
        gamma = jnp.ones((E, H), dtype=jnp.float32)
        beta = jnp.zeros((E, H), dtype=jnp.float32)
        return {'input_tensor': x, 'expert_idx': expert_idx, 'Wi': Wi, 'bi': bi, 'Wo': Wo, 'bo': bo, 'gamma': gamma, 'beta': beta}
    _L2_cond_all = _L2_cond_setup()
    _L2_cond_in = {k: v for k, v in _L2_cond_all.items() if k in ('Wi', 'bi', 'Wo', 'bo', 'gamma', 'beta')}
    del _L2_cond_all

    def _L3_cond_setup():
        import jax, jax.numpy as jnp
        import numpy as np
        B, NX, NY = (16, 512, 512)

        def _grad(f, axis):
            fm = jnp.moveaxis(f, axis, -1)
            g = (jnp.roll(fm, -1, -1) - jnp.roll(fm, 1, -1)) * 0.5
            g0 = (-3.0 * fm[..., 0] + 4.0 * fm[..., 1] - fm[..., 2]) * 0.5
            gN = (3.0 * fm[..., -1] - 4.0 * fm[..., -2] + fm[..., -3]) * 0.5
            g = g.at[..., 0].set(g0).at[..., -1].set(gN)
            return jnp.moveaxis(g, -1, axis)

        def _grad2(f, axis):
            fm = jnp.moveaxis(f, axis, -1)
            g = jnp.roll(fm, -1, -1) - 2.0 * fm + jnp.roll(fm, 1, -1)
            g0 = 2.0 * fm[..., 0] - 5.0 * fm[..., 1] + 4.0 * fm[..., 2] - fm[..., 3]
            gN = 2.0 * fm[..., -1] - 5.0 * fm[..., -2] + 4.0 * fm[..., -3] - fm[..., -4]
            g = g.at[..., 0].set(g0).at[..., -1].set(gN)
            return jnp.moveaxis(g, -1, axis)
        key = jax.random.key(seed)
        k1, k2, k3, k4 = jax.random.split(key, 4)
        f = jax.random.uniform(k1, (B, NX, NY), dtype=jnp.float32)
        A_grid = jax.random.normal(k2, (2, NX, NY), dtype=jnp.float32)
        B_grid = jax.random.uniform(k3, (3, NX, NY), dtype=jnp.float32)
        dt = jax.random.uniform(k4, (B,), dtype=jnp.float32)
        return {'f': f, 'A_grid': A_grid, 'B_grid': B_grid, 'dt': dt}
    _L3_cond_all = _L3_cond_setup()
    _L3_cond_in = {k: v for k, v in _L3_cond_all.items() if k in ('A_grid', 'B_grid')}
    del _L3_cond_all
    return {'x': x, 'itok_B_0_15': itok_B_0_15, 'itok_B_34_63': itok_B_34_63, 'fside_Bx16xSxS_0': fside_Bx16xSxS_0, 'itok_B_0_7': itok_B_0_7, 'condB_dt': condB_dt, 'mask_Bx1xSxS_bk0': mask_Bx1xSxS_bk0, 'L0_cond_down_W': _L0_cond_in['down_W'], 'L0_cond_down_b': _L0_cond_in['down_b'], 'L0_cond_up_W': _L0_cond_in['up_W'], 'L0_cond_up_b': _L0_cond_in['up_b'], 'L0_cond_expert_W': _L0_cond_in['expert_W'], 'L0_cond_expert_b': _L0_cond_in['expert_b'], 'L0_cond_domain_emb': _L0_cond_in['domain_emb'], 'L0_cond_ln_gamma': _L0_cond_in['ln_gamma'], 'L0_cond_ln_beta': _L0_cond_in['ln_beta'], 'L1_cond_W_ada': _L1_cond_in['W_ada'], 'L1_cond_b_ada': _L1_cond_in['b_ada'], 'L1_cond_Wq': _L1_cond_in['Wq'], 'L1_cond_bq': _L1_cond_in['bq'], 'L1_cond_Wk': _L1_cond_in['Wk'], 'L1_cond_bk': _L1_cond_in['bk'], 'L1_cond_Wv': _L1_cond_in['Wv'], 'L1_cond_bv': _L1_cond_in['bv'], 'L1_cond_Wo': _L1_cond_in['Wo'], 'L1_cond_bo': _L1_cond_in['bo'], 'L1_cond_W1': _L1_cond_in['W1'], 'L1_cond_b1': _L1_cond_in['b1'], 'L1_cond_W2': _L1_cond_in['W2'], 'L1_cond_b2': _L1_cond_in['b2'], 'L1_cond_g2': _L1_cond_in['g2'], 'L1_cond_beta2': _L1_cond_in['beta2'], 'L2_cond_Wi': _L2_cond_in['Wi'], 'L2_cond_bi': _L2_cond_in['bi'], 'L2_cond_Wo': _L2_cond_in['Wo'], 'L2_cond_bo': _L2_cond_in['bo'], 'L2_cond_gamma': _L2_cond_in['gamma'], 'L2_cond_beta': _L2_cond_in['beta'], 'L3_cond_A_grid': _L3_cond_in['A_grid'], 'L3_cond_B_grid': _L3_cond_in['B_grid']}

def reference(x, itok_B_0_15, itok_B_34_63, fside_Bx16xSxS_0, itok_B_0_7, condB_dt, mask_Bx1xSxS_bk0, L0_cond_down_W, L0_cond_down_b, L0_cond_up_W, L0_cond_up_b, L0_cond_expert_W, L0_cond_expert_b, L0_cond_domain_emb, L0_cond_ln_gamma, L0_cond_ln_beta, L1_cond_W_ada, L1_cond_b_ada, L1_cond_Wq, L1_cond_bq, L1_cond_Wk, L1_cond_bk, L1_cond_Wv, L1_cond_bv, L1_cond_Wo, L1_cond_bo, L1_cond_W1, L1_cond_b1, L1_cond_W2, L1_cond_b2, L1_cond_g2, L1_cond_beta2, L2_cond_Wi, L2_cond_bi, L2_cond_Wo, L2_cond_bo, L2_cond_gamma, L2_cond_beta, L3_cond_A_grid, L3_cond_B_grid):
    import jax
    import jax.numpy as jnp

    def _L0_cond_ref(hidden_states, domain_id, down_W, down_b, up_W, up_b, expert_W, expert_b, domain_emb, ln_gamma, ln_beta):
        import jax, jax.numpy as jnp
        import numpy as np
        B, S, D = (32, 512, 512)
        A = 128
        E = 16
        LN_EPS = 1e-05
        residual = hidden_states
        hidden = jnp.einsum('bsd,ad->bsa', hidden_states, down_W) + down_b
        hidden = jax.nn.gelu(hidden, approximate=False)
        valid = (domain_id >= 0) & (domain_id < E)
        idx = jnp.clip(domain_id, 0, E - 1)
        Wsel = expert_W[idx]
        bsel = expert_b[idx]
        expert_out = jnp.einsum('bsa,boa->bso', hidden, Wsel) + bsel[:, None, :]
        domain_output = jnp.where(valid[:, None, None], expert_out, hidden)
        hidden = domain_output + domain_emb[idx][:, None, :]
        hidden = jnp.einsum('bsa,da->bsd', hidden, up_W) + up_b
        x = hidden + residual
        mu = jnp.mean(x, axis=-1, keepdims=True)
        var = jnp.mean(jnp.square(x - mu), axis=-1, keepdims=True)
        return (x - mu) * jax.lax.rsqrt(var + LN_EPS) * ln_gamma + ln_beta

    def _L1_cond_ref(src, src_mask, timestep, attention_bias, W_ada, b_ada, Wq, bq, Wk, bk, Wv, bv, Wo, bo, W1, b1, W2, b2, g2, beta2):
        import jax, jax.numpy as jnp
        import numpy as np
        import math
        D_MODEL = 512
        N_HEAD = 16
        HEAD_DIM = D_MODEL // N_HEAD
        D_FF = 2048
        NUM_STEPS = 100.0
        RESCALE = 4000.0
        EPS = 1e-05

        def _sin_emb(t):
            half = D_MODEL // 2
            x = t.astype(jnp.float32) / NUM_STEPS * RESCALE
            freqs = jnp.exp(jnp.arange(half, dtype=jnp.float32) * (-math.log(10000.0) / (half - 1)))
            e = x[:, None] * freqs[None, :]
            return jnp.concatenate([jnp.sin(e), jnp.cos(e)], axis=-1)

        def _ln(x):
            m = jnp.mean(x, axis=-1, keepdims=True)
            v = jnp.var(x, axis=-1, keepdims=True)
            return (x - m) / jnp.sqrt(v + EPS)

        def _gelu2(x):
            return x * jax.nn.sigmoid(1.702 * x)
        B, S, D = src.shape
        emb = jax.nn.silu(_sin_emb(timestep)) @ W_ada + b_ada
        scale, shift = jnp.split(emb[:, None, :], 2, axis=-1)
        x = _ln(src) * (1.0 + scale) + shift
        q = (x @ Wq + bq).reshape(B, S, N_HEAD, HEAD_DIM).transpose(0, 2, 1, 3)
        k = (x @ Wk + bk).reshape(B, S, N_HEAD, HEAD_DIM).transpose(0, 2, 1, 3)
        v = (x @ Wv + bv).reshape(B, S, N_HEAD, HEAD_DIM).transpose(0, 2, 1, 3)
        scores = jnp.einsum('bhqd,bhkd->bhqk', q / math.sqrt(HEAD_DIM), k)
        scores = scores + attention_bias
        scores = jnp.where(src_mask, -jnp.inf, scores.astype(jnp.float32))
        probs = jax.nn.softmax(scores, axis=-1).astype(v.dtype)
        ctx = jnp.einsum('bhqk,bhkd->bhqd', probs, v)
        ctx = ctx.transpose(0, 2, 1, 3).reshape(B, S, D)
        x = x + (ctx @ Wo + bo)
        h = _ln(x) * g2 + beta2
        ff = _gelu2(h @ W1 + b1) @ W2 + b2
        return x + ff

    def _L2_cond_ref(input_tensor, expert_idx, Wi, bi, Wo, bo, gamma, beta):
        import jax, jax.numpy as jnp
        import numpy as np
        E, H, I = (8, 512, 2048)
        B, S = (4, 512)
        LN_EPS = 1e-12
        Wi_b = Wi[expert_idx]
        bi_b = bi[expert_idx]
        Wo_b = Wo[expert_idx]
        bo_b = bo[expert_idx]
        g_b = gamma[expert_idx]
        be_b = beta[expert_idx]
        h = jax.nn.gelu(jnp.einsum('bsh,bhi->bsi', input_tensor, Wi_b) + bi_b[:, None, :], approximate=False)
        o = jnp.einsum('bsi,bih->bsh', h, Wo_b) + bo_b[:, None, :]
        r = o + input_tensor
        mu = jnp.mean(r, axis=-1, keepdims=True)
        var = jnp.mean(jnp.square(r - mu), axis=-1, keepdims=True)
        y = (r - mu) * jax.lax.rsqrt(var + LN_EPS)
        return y * g_b[:, None, :] + be_b[:, None, :]

    def _L3_cond_ref(f, A_grid, B_grid, dt):
        import jax, jax.numpy as jnp
        import numpy as np
        B, NX, NY = (16, 512, 512)

        def _grad(f, axis):
            fm = jnp.moveaxis(f, axis, -1)
            g = (jnp.roll(fm, -1, -1) - jnp.roll(fm, 1, -1)) * 0.5
            g0 = (-3.0 * fm[..., 0] + 4.0 * fm[..., 1] - fm[..., 2]) * 0.5
            gN = (3.0 * fm[..., -1] - 4.0 * fm[..., -2] + fm[..., -3]) * 0.5
            g = g.at[..., 0].set(g0).at[..., -1].set(gN)
            return jnp.moveaxis(g, -1, axis)

        def _grad2(f, axis):
            fm = jnp.moveaxis(f, axis, -1)
            g = jnp.roll(fm, -1, -1) - 2.0 * fm + jnp.roll(fm, 1, -1)
            g0 = 2.0 * fm[..., 0] - 5.0 * fm[..., 1] + 4.0 * fm[..., 2] - fm[..., 3]
            gN = 2.0 * fm[..., -1] - 5.0 * fm[..., -2] + 4.0 * fm[..., -3] - fm[..., -4]
            g = g.at[..., 0].set(g0).at[..., -1].set(gN)
            return jnp.moveaxis(g, -1, axis)
        Af = A_grid[None] * f[:, None]
        Bf = B_grid[None] * f[:, None]
        gradv_Af = _grad(Af[:, 0], 1) + _grad(Af[:, 1], 2)
        gradvv_Bf = _grad2(Bf[:, 0], 1) + _grad2(Bf[:, 1], 2) + _grad(_grad(Bf[:, 2], 2), 1) + _grad(_grad(Bf[:, 2], 1), 2)
        df = -gradv_Af + gradvv_Bf * 0.5
        f_new = f + df * dt[:, None, None]
        return jnp.maximum(f_new, 0.0)
    x = _L0_cond_ref(x, itok_B_0_15, L0_cond_down_W, L0_cond_down_b, L0_cond_up_W, L0_cond_up_b, L0_cond_expert_W, L0_cond_expert_b, L0_cond_domain_emb, L0_cond_ln_gamma, L0_cond_ln_beta)
    x = _L1_cond_ref(x, mask_Bx1xSxS_bk0, itok_B_34_63, fside_Bx16xSxS_0, L1_cond_W_ada, L1_cond_b_ada, L1_cond_Wq, L1_cond_bq, L1_cond_Wk, L1_cond_bk, L1_cond_Wv, L1_cond_bv, L1_cond_Wo, L1_cond_bo, L1_cond_W1, L1_cond_b1, L1_cond_W2, L1_cond_b2, L1_cond_g2, L1_cond_beta2)
    x = _L2_cond_ref(x, itok_B_0_7, L2_cond_Wi, L2_cond_bi, L2_cond_Wo, L2_cond_bo, L2_cond_gamma, L2_cond_beta)
    x = _L3_cond_ref(x, L3_cond_A_grid, L3_cond_B_grid, condB_dt)
    return x

_drawn_inputs = setup_inputs


def setup_inputs(seed=0):
    import zlib

    import numpy as np

    out = dict(_drawn_inputs(seed))
    spreads = {'L0_cond_ln_gamma': (1.0, 0.2),
     'L0_cond_ln_beta': (0.0, 0.1),
     'L1_cond_b_ada': (0.0, 0.1),
     'L1_cond_bq': (0.0, 0.8),
     'L1_cond_bk': (0.0, 0.8),
     'L1_cond_bv': (0.0, 0.1),
     'L1_cond_bo': (0.0, 0.1),
     'L1_cond_b1': (0.0, 0.1),
     'L1_cond_b2': (0.0, 0.1),
     'L1_cond_g2': (1.0, 0.2),
     'L1_cond_beta2': (0.0, 0.334),
     'L2_cond_bi': (0.0, 0.1),
     'L2_cond_bo': (0.0, 0.1),
     'L2_cond_gamma': (1.0, 0.2),
     'L2_cond_beta': (0.0, 0.1)}
    factors = {'fside_Bx16xSxS_0': 5.446, 'L0_cond_down_b': 8.0, 'L1_cond_Wq': 8.0, 'L1_cond_Wk': 8.0}
    for name, (base, spread) in spreads.items():
        noise = np.random.default_rng([zlib.crc32(name.encode()), seed]).standard_normal(out[name].shape)
        drawn = base * np.exp(spread * noise) if base else spread * noise
        out[name] = jnp.asarray(drawn.astype(out[name].dtype))
    for name, factor in factors.items():
        out[name] = (out[name] * factor).astype(out[name].dtype)
    return out
```

```python
import math
from contextlib import ExitStack

import numpy as np

import concourse.bass as bass
from concourse import mybir

ALU = mybir.AluOpType
ACT = mybir.ActivationFunctionType
F32 = mybir.dt.float32
F16 = mybir.dt.float16
BF16 = mybir.dt.bfloat16
I32 = mybir.dt.int32
U8 = mybir.dt.uint8

LINKS_A = 60
LINKS_B = 146
P = 128
B, S, D = 8, 512, 512
T = S // P
C = D // P
NE0, A = 16, 128
H, HD = 16, 32
G = H // 4
FF = 2048
NF = FF // P
NE2 = 8
WS = 256.0
NEG = -1.0e30
PS = 4096.0
RSQRT_SEED = 1597463007.0
MAGIC = 12582912.0
TWO_PI = (6.28125, 0.0019350051879882812, 3.0199159819567e-07)


class Banks:

    def __init__(self, order, unsignalled=()):
        self.uses = [0] * 8
        self.place = {}
        last = {bank: key for key, bank in order}
        self.first, seen = {}, set()
        for key, bank in order:
            self.first[key] = bank not in seen
            seen.add(bank)
            self.place[key] = (bank, self.uses[bank], last[bank])
            self.uses[bank] += key[0] not in unsignalled
            last[bank] = key


def rsqrt_steps(dve, link, v, y, a, seed_bits, v_bits):
    link(dve.tensor_scalar(seed_bits, v_bits, -0.5, RSQRT_SEED, ALU.mult, ALU.add))
    for _ in range(3):
        link(dve.tensor_tensor(a, y, y, ALU.mult))
        link(dve.scalar_tensor_tensor(out=a, in0=a, scalar=-0.5, in1=v, op0=ALU.mult, op1=ALU.mult))
        link(dve.scalar_tensor_tensor(out=y, in0=a, scalar=1.5, in1=y, op0=ALU.add, op1=ALU.mult))


def ada_embedding(nc, a, ada_rows):
    with ExitStack() as ctx:
        def sb(name, shape, dt):
            return ctx.enter_context(nc.sbuf_tensor(name, shape, dt))

        def sem(name):
            return ctx.enter_context(nc.semaphore(name))

        steps_i = sb("steps_i", [P, B], I32)
        steps = sb("steps", [P, B], F32)
        freq = sb("freq", [P, 2], F32)
        ang = sb("ang", [P, C, B], F32)
        turns = sb("turns", [P, C, B], F32)
        emb = sb("emb", [P, C, B], F32)
        w_ada = sb("w_ada", [P, C, 2 * D], F32)
        b_ada = sb("b_ada", [B, 2 * D], F32)
        rows = sb("rows", [B, 2 * D], F32)
        acc = [ctx.enter_context(nc.psum_tensor(f"ada_acc{i}", [P, D], F32)) for i in range(2)]
        inputs_in = sem("ada_inputs_in")
        chain = sem("ada_dve_chain")
        reduced = sem("ada_angles_reduced")
        act_done = sem("ada_act_done")
        acc_full = sem("ada_acc_full")
        rows_ready = sem("ada_rows_ready")
        rows_out = sem("ada_rows_out")
        block = ctx.enter_context(nc.Block())

        @block.sync
        def _(sp):
            sp.dma_start(steps_i[:, :], a["steps"].partition_broadcast(P)).then_inc(inputs_in, 16)
            sp.dma_start(freq[:, :], a["freqs"]).then_inc(inputs_in, 16)
            sp.dma_start(w_ada[:, :, :], a["W_ada"].rearrange("(c p) n -> p c n", p=P)).then_inc(inputs_in, 16)
            sp.dma_start(b_ada[:, :], a["b_ada"].partition_broadcast(B)).then_inc(inputs_in, 16)
            sp.wait_ge(rows_ready, 3)
            sp.dma_start(ada_rows, rows[:, :]).then_inc(rows_out, 16)
            sp.wait_ge(rows_out, 16)

        @block.vector
        def _(dve):
            n = [0]

            def link(ins):
                n[0] += 1
                ins.then_inc(chain, 1)
                dve.wait_ge(chain, n[0])

            dve.wait_ge(inputs_in, 64)
            link(dve.tensor_copy(steps[:, :], steps_i[:, :]))
            link(dve.tensor_scalar(steps[:, :], steps[:, :], 40.0, None, ALU.mult))
            for c in range(2):
                link(dve.tensor_scalar(ang[:, c, :], steps[:, :], freq[:, c:c + 1], None, ALU.mult))
            lo, k = ang[:, 0:2, :], turns[:, 0:2, :]
            link(dve.tensor_scalar(k, lo, 1.0 / (2.0 * math.pi), MAGIC, ALU.mult, ALU.add))
            link(dve.tensor_scalar(k, k, MAGIC, None, ALU.subtract))
            for part in TWO_PI:
                link(dve.scalar_tensor_tensor(out=lo, in0=k, scalar=-part, in1=lo, op0=ALU.mult, op1=ALU.add))
            hi, over = ang[:, 2:4, :], turns[:, 2:4, :]
            link(dve.tensor_scalar(hi, lo, math.pi / 2, None, ALU.add))
            link(dve.tensor_scalar(over, hi, math.pi, -2.0 * math.pi, ALU.is_gt, ALU.mult))
            link(dve.tensor_tensor(hi, hi, over, ALU.add))
            dve.tensor_scalar(ang[:, :, :], ang[:, :, :], -3.1415925, 3.1415925, ALU.max, ALU.min).then_inc(reduced, 1)
            for i in range(2):
                dve.wait_ge(acc_full, i + 1)
                dve.tensor_tensor(rows[:, i * D:(i + 1) * D], acc[i][0:B, :], b_ada[:, i * D:(i + 1) * D],
                                  ALU.add).then_inc(rows_ready, 1)
            dve.wait_ge(rows_ready, 2)
            dve.tensor_scalar(rows[:, 0:D], rows[:, 0:D], 1.0, None, ALU.add).then_inc(rows_ready, 1)

        @block.scalar
        def _(act):
            act.wait_ge(reduced, 1)
            act.activation(ang[:, :, :], ang[:, :, :], ACT.Sin).then_inc(act_done, 1)
            act.wait_ge(act_done, 1)
            act.activation(emb[:, :, :], ang[:, :, :], ACT.Silu).then_inc(act_done, 1)

        @block.tensor
        def _(pe):
            pe.wait_ge(act_done, 2)
            pe.wait_ge(inputs_in, 64)
            for i in range(2):
                for c in range(C):
                    mm = pe.matmul(acc[i][0:B, :], emb[:, c, :], w_ada[:, c, i * D:(i + 1) * D],
                                   start=(c == 0), stop=(c == C - 1))
                mm.then_inc(acc_full, 1)


HT = H * T
LAG_T = 5
LAG_PV = 7
SLOTS_ALL = HT + 10


def rinv_slot(g):
    return 4 * T * (g + 1) + 1


def turn_slot(g):
    return 4 * T * (g + 1) + 2


def ctx_slot(g):
    return 4 * T * (g + 1) + LAG_PV + 1


PE_L0 = {3: ("down",), 7: ("expert",)} | {9 + 2 * t: ("up", t) for t in range(T)}
ACT_L0 = {4: ("down",), 8: ("expert",)} | {26 + 2 * t: ("scale0", t) for t in range(T)} \
    | {45 + 2 * t: ("scale1", t) for t in range(T)}
DVE_L0 = {4: ("g",), 8: ("e",)} | {10 + 2 * t: ("y", t) for t in range(T)} \
    | {18 + 2 * t: ("stats0", t) for t in range(T)} | {25: ("rstd",)} \
    | {37 + 2 * t: ("stats1", t) for t in range(T)} | {44: ("rstd",)}


def attention_slots():
    order, ring = [], 0
    for n in range(SLOTS_ALL):
        if n < HT:
            order.append((("S", n // T, n % T), n % 3))
        if n in PE_L0:
            order.append((PE_L0[n], 3 + ring % 3))
            ring += 1
        if 0 <= n - LAG_T < HT:
            m = n - LAG_T
            order.append((("T", m // T, m % T), 3 + ring % 3))
            ring += 1
        if 0 <= n - LAG_PV < HT and (n - LAG_PV) % (4 * T) == 0:
            g = (n - LAG_PV) // (4 * T)
            order.append((("ctx", g), 6 + g % 2))
        for g in range(G):
            if n == turn_slot(g):
                order.append((("R", g), 3 + ring % 3))
                ring += 1
    return order


def attention_pass(nc, a, ada_rows, x2_dram):
    order = [(("x1T", c), 4 + c) for c in range(C)]
    order += [(("q", c), c) for c in range(C)]
    order += [(("k", c), 4 + c) for c in range(C)]
    order += [(("v", t), t) for t in range(T)]
    order += [(("xT", c), 4 + c) for c in range(C)]
    order += attention_slots()
    order += [(("wo", t), t) for t in range(T)]
    banks = Banks(order, ("ctx",))

    with ExitStack() as ctx:
        def sb(name, shape, dt):
            return ctx.enter_context(nc.sbuf_tensor(name, shape, dt))

        def sem(name):
            return ctx.enter_context(nc.semaphore(name))

        wq, wk, wv, wo = ([sb(f"w{n}_{h}", [P, C, D], F16) for h in ("hi", "lo")] for n in "qkvo")
        wdown = [sb(f"wdown_{h}", [P, C, A], F16) for h in ("hi", "lo")]
        wup = [sb(f"wup_{h}", [P, D], F16) for h in ("hi", "lo")]
        wexp = [sb(f"wexp_{h}", [P, A], F16) for h in ("hi", "lo")]
        ident = sb("ident", [P, P], F32)
        ident_bf = sb("ident_bf", [P, P], BF16)
        down_b = sb("down_b", [P, 1], F32)
        bq, bk, bv = (sb(f"b{n}", [P, C], F32) for n in "qkv")
        up_b, ln_g, ln_b, bo = (sb(n, [P, D], F32) for n in ("up_b", "ln_g", "ln_b", "bo"))
        ada = sb("ada", [P, 2, D], F32)
        dom = sb("dom", [P, B], I32)
        dom_f = sb("dom_f", [P, B], F32)
        valid = sb("valid", [P, B], F32)
        invalid = sb("invalid", [P, B], F32)
        dom_at = sb("dom_at", [1, B], I32)
        exp_raw = sb("exp_raw", [P, A], F32)
        exp_eff = sb("exp_eff", [P, A], F32)
        exp_vec = sb("exp_vec", [P, 2], F32)
        exp_bias = sb("exp_bias", [P, 1], F32)
        xin = sb("xin", [P, T, D], F32)
        x1 = sb("x1", [P, T, D], F32)
        xT = [sb(f"xT_{h}", [P, C, S], F16) for h in ("hi", "lo")]
        q_st = sb("q_st", [P, H, S], F16)
        k_st = sb("k_st", [P, H, S], F16)
        v_pad = [sb(f"v_{h}", [P, T, H, P], F16) for h in ("hi", "lo")]
        mask_raw = sb("mask_raw", [P, T, S], U8)
        mask_add = sb("mask_add", [P, T, S], BF16)
        NB = 4
        bias = sb("bias", [P, NB, 2, S], F32)
        NT = 4
        negs = sb("negs", [P, NT, S], F32)
        nmax = sb("nmax", [P, 2, T], F32)
        rsum = sb("rsum", [P, T, H], F32)
        rinv = sb("rinv", [P, T, 4], F32)
        rinv_x = sb("rinv_x", [P, T, P], F32)
        rinv_T = sb("rinv_T", [P, S], F32)
        ctx32 = sb("ctx32", [P, S], F32)
        prob = sb("prob", [P, 2, T, S], F32)
        pT = [sb(f"pT_{h}", [P, 2, T, S], F16) for h in ("hi", "lo")]
        qT = [pT[h][:, 0, :, :] for h in range(2)]
        kT = [pT[h][:, 1, :, :] for h in range(2)]
        hid32 = rinv_T
        hT = [ctx32[:, h * D // 2:(h + 1) * D // 2].bitcast(F16) for h in range(2)]
        f32t = negs
        raw = prob
        stats = sb("stats", [P, T, 6], F32)
        mv = sb("mv", [P, T, 2], F32)
        var = sb("var", [P, T], F32)
        rstd = sb("rstd", [P, T], F32)
        shift = sb("shift", [P, T], F32)
        newt = sb("newt", [P, T], F32)

        psum = [ctx.enter_context(nc.psum_tensor(f"bank{i}", [P, S], F32)) for i in range(8)]
        full = [sem(f"bank{i}_full") for i in range(8)]

        raw_in = [sem(f"raw{i}_in") for i in range(2)]
        vec_in = sem("vec_in")
        dom_in = sem("dom_in")
        dom_clipped = sem("dom_clipped")
        ident_set = sem("ident_set")
        weights_split = sem("weights_split")
        v_zeroed = sem("v_zeroed")
        x_in = sem("x_in")
        mask_in = sem("mask_in")
        expert_in = sem("expert_in")
        ada_in = sem("ada_in")
        bias_in = [sem(f"bias{i}_in") for i in range(NB)]
        mask_ready = sem("mask_ready")
        expert_ready = sem("expert_ready")
        hi_done = sem("hi_done")
        x_hi = sem("x_hi")
        first_full = sem("first_tiles_full")
        weights_hi = sem("weights_hi")
        hid_ready = sem("hid_ready")
        pool_chain = sem("pool_chain")
        xT_split = sem("xT_split")
        x1T_split = sem("x1T_split")
        f32_ready = sem("f32_ready")
        g_split = sem("g_split")
        e_split = sem("e_split")
        qk_split = sem("qk_split")
        v_split = sem("v_split")
        qk_stacked = sem("qk_stacked")
        xb_ready = sem("xb_ready")
        y_ready = sem("y_ready")
        scored = sem("scored")
        rstd_ready = sem("rstd_ready")
        scaled0 = sem("scaled0")
        ln0_ready = sem("ln0_ready")
        scaled1 = sem("scaled1")
        x1_ready = sem("x1_ready")
        x1b_ready = sem("x1b_ready")
        prob_ready = sem("prob_ready")
        pT_split = sem("pT_split")
        pv_done = sem("pv_done")
        rinv_ready = sem("rinv_ready")
        rinv_T_ready = sem("rinv_T_ready")
        ctx_ready = sem("ctx_ready")
        ctx_hi = sem("ctx_hi")
        ctx_split = sem("ctx_split")
        x2_ready = sem("x2_ready")
        x2_out = sem("x2_out")
        chain = sem("dve_chain")
        carrier = sem("wait_carrier")

        block = ctx.enter_context(nc.Block())

        BEGUN = {"vector": (x2_ready, pT_split, ctx_ready, scored, v_split, ctx_split),
                 "scalar": (x2_out, prob_ready), "tensor": (pv_done,)}
        base = {s: 1 for sems in BEGUN.values() for s in sems}
        base |= {xT_split: C, hid_ready: 2, y_ready: T}

        def begin(eng, name):
            for s in BEGUN[name]:
                eng.sem_inc(s, 1)

        def read_by(key):
            name, k = key[0], key[-1]
            return {"xT": (xT_split, C, k), "down": (hid_ready, 2, 0), "expert": (hid_ready, 2, 1),
                    "up": (y_ready, T, k), "x1T": (x1T_split, C, k), "q": (f32_ready, 12, 0),
                    "k": (f32_ready, 12, 4), "v": (f32_ready, 12, 8), "S": (scored, H * T, k),
                    "T": (pT_split, H * T, k), "R": (rinv_T_ready, G, k), "ctx": (ctx_ready, G, k),
                    "wo": (x2_ready, T, k)}[name]

        def claim(pe, it, key):
            bank, _, last = banks.place[key]
            signal, per, k = read_by(last)
            if last[0] in ("q", "k", "v"):
                k += last[1]
            if last[0] in ("S", "T"):
                k += last[1] * T
            pe.wait_ge(signal, base.get(signal, 0) + it * per + (0 if banks.first[key] else k + 1))
            return psum[bank]

        def arrived(eng, it, key):
            bank, before, _ = banks.place[key]
            eng.wait_ge(full[bank], it * banks.uses[bank] + before + 1)
            return psum[bank]

        def full_of(key):
            return full[banks.place[key][0]]

        def f32_split(n):
            return (qk_split, 2 * C, n + 1) if n < 8 else (v_split, T, n - 7)

        FIRST = [("xT", c) for c in range(C)] + [("down",), ("expert",)] + [("up", t) for t in range(T)]
        FIRST_BANK = {key: i if i < 6 else i - 6 for i, key in enumerate(FIRST)}

        def before_it(it):
            return 0 if it is None else it + 1

        def l0_tile(eng, it, key):
            if it is None:
                eng.wait_ge(first_full, FIRST.index(key) + 1)
                return psum[FIRST_BANK[key]]
            return arrived(eng, it, key)

        WEIGHTS = [("down_WT", wdown), ("up_WT", wup), ("Wq", wq), ("Wk", wk), ("Wv", wv), ("Wo", wo)]
        VECS = [(down_b[:, :], a["down_b"]), (bq[:, :], a["bq"]), (bk[:, :], a["bk"]), (bv[:, :], a["bv"]),
                (up_b[:, :], a["up_b"].partition_broadcast(P)), (ln_g[:, :], a["ln_g"].partition_broadcast(P)),
                (ln_b[:, :], a["ln_b"].partition_broadcast(P)), (bo[:, :], a["bo"].partition_broadcast(P))]
        SLOTS = [(0, 0, 0), (1, 1, 0), (2, 0, 1)]

        def weight_view(tile):
            return tile[:, :, :] if len(tile.shape) == 3 else tile[:, :]

        def raw_view(i, tile):
            n = tile.shape[-1] * (tile.shape[1] if len(tile.shape) == 3 else 1)
            v = raw[:, i % 2, :, :].rearrange("p t s -> p (t s)")[:, 0:n]
            return v.rearrange("p (c n) -> p c n", c=tile.shape[1]) if len(tile.shape) == 3 else v

        @block.sync
        def _(sp):
            sp.dma_start(dom[:, :], a["dom"].partition_broadcast(P)).then_inc(dom_in, 16)

            def load_x(seq):
                sp.dma_start(xin[:, :, :], a["x"][seq].rearrange("(t p) d -> p t d", p=P)).then_inc(x_in, 16)

            def load_expert(at):
                e = sp.value_load(dom_at[0:1, at], min_val=0, max_val=NE0 - 1)
                sp.dma_start(exp_raw[:, :], a["exp_WT"][e]).then_inc(expert_in, 16)
                sp.dma_start(exp_vec[:, :], a["exp_vec"][e]).then_inc(expert_in, 16)

            def load_ada(seq):
                sp.dma_start(ada[:, :, :], ada_rows[seq].rearrange("(k d) -> k d", k=2).partition_broadcast(P)).then_inc(ada_in, 16)

            def load_mask(seq):
                sp.dma_start(mask_raw[:, :, :], a["mask"][seq].rearrange("(t p) s -> p t s", p=P)).then_inc(mask_in, 16)

            def load_weight(i):
                name, (hi, _) = WEIGHTS[i]
                if i >= 2:
                    sp.wait_ge(weights_split, i - 1)
                src = a[name]
                if len(hi.shape) == 3 and name != "down_WT":
                    src = src.rearrange("(c p) n -> p c n", p=P)
                sp.dma_start(raw_view(i, hi), src).then_inc(raw_in[i % 2], 16)

            load_x(0)
            load_weight(0)
            load_weight(1)
            sp.wait_ge(dom_clipped, 1)
            load_expert(slice(0, 1))
            for dst, src in VECS:
                sp.dma_start(dst, src).then_inc(vec_in, 16)
            load_ada(0)
            load_mask(0)
            for i in range(2, len(WEIGHTS)):
                load_weight(i)
            with sp.Fori(0, B) as it:
                nxt = (it + 1) % B

                def load_bias(n):
                    sp.wait_ge(scored, 1 + it * (T * H) + max(0, 2 * (n - NB) + 2))
                    h, j = n // 2, n % 2
                    src = a["bias"][it, h, j * 2 * P:(j + 1) * 2 * P, :].rearrange("(t p) s -> p t s", p=P)
                    sp.dma_start(bias[:, n % NB, :, :], src).then_inc(bias_in[n % NB], 16)

                for n in range(NB):
                    load_bias(n)
                sp.wait_ge(x1b_ready, it * T + T)
                arrived(sp, it, ("x1T", C - 1))
                load_x(nxt)
                sp.wait_ge(x1_ready, it * T + T)
                load_expert(bass.ds(nxt, 1))
                load_ada(nxt)
                sp.wait_ge(mask_ready, it * 1 + 1)
                load_mask(nxt)
                for which, (parts, stack) in enumerate(((qT, q_st), (kT, k_st))):
                    sp.wait_ge(qk_split, it * 2 * C + (which + 1) * C)
                    for i in range(4):
                        for slot in SLOTS:
                            sp.dma_start(
                                stack[32 * slot[0]:32 * slot[0] + 32, :, :].rearrange("p (c i) s -> p i c s", i=4)[:, i],
                                parts[slot[1 + which]][32 * i:32 * i + 32, :, :]).then_inc(qk_stacked, 16)
                for n in range(NB, 2 * H):
                    load_bias(n)

        @block.gpsimd
        def _(pool):
            pool.memset(ident[:, :], 0.0).then_inc(ident_set, 1)
            pool.wait_ge(ident_set, 1)
            pool.affine_select(out=ident[:, :], in_=ident[:, :], compare_op=ALU.not_equal, fill=1.0, base=0,
                               pattern=[[-1, P]], channel_multiplier=1).then_inc(ident_set, 1)
            pool.wait_ge(ident_set, 2)
            pool.tensor_copy(ident_bf[:, :], ident[:, :]).then_inc(ident_set, 1)
            for part in v_pad:
                pool.memset(part[:, :, :, :].rearrange("p t h m -> p (t h m)").bitcast(F32), 0.0).then_inc(v_zeroed, 1)
            pool.wait_ge(vec_in, 16 * len(VECS))
            steps = [0]

            def pool_link(base, ins):
                steps[0] += 1
                ins.then_inc(pool_chain, 1)
                pool.wait_ge(pool_chain, base + steps[0])

            def finish_x1(it):
                q = before_it(it)
                base = 0 if it is None else q * (2 * T)
                steps[0] = 0
                pool.wait_ge(x_in, q * 16 + 16)
                l0_tile(pool, it, ("xT", C - 1))
                for t in range(T):
                    pool.tensor_tensor(xin[:, t, :], xin[:, t, :], up_b[:, :], ALU.add).then_inc(xb_ready, 1)
                for t in range(T):
                    pool.wait_ge(scaled0, q * T + t + 1)
                    pool_link(base, pool.tensor_tensor(xin[:, t, :], xin[:, t, :], ln_g[:, :], ALU.mult))
                    pool.tensor_tensor(xin[:, t, :], xin[:, t, :], ln_b[:, :], ALU.add).then_inc(ln0_ready, 1)
                pool.wait_ge(ada_in, q * 16 + 16)
                for t in range(T):
                    pool.wait_ge(scaled1, q * T + t + 1)
                    pool_link(base, pool.tensor_tensor(xin[:, t, :], xin[:, t, :], ada[:, 0, :], ALU.mult))
                    pool.tensor_tensor(xin[:, t, :], xin[:, t, :], ada[:, 1, :], ALU.add).then_inc(x1_ready, 1)

            finish_x1(None)
            with pool.Fori(0, B) as it:
                pool.wait_ge(x2_out, 1 + it * 64)
                for t in range(T):
                    pool.wait_ge(x1_ready, it * T + t + 1)
                    pool.tensor_tensor(x1[:, t, :], xin[:, t, :], bo[:, :], ALU.add).then_inc(x1b_ready, 1)
                finish_x1(it)

        @block.tensor
        def _(pe):
            begin(pe, "tensor")
            pe.wait_ge(ident_set, 3)

            def three(out, w, x, first, last):
                pe.matmul(out, w[0], x[0], start=first, stop=False)
                pe.matmul(out, w[0], x[1], start=False, stop=False)
                return pe.matmul(out, w[1], x[0], start=False, stop=last)

            def transposes(bank, c):
                for t in range(T):
                    mm = pe.transpose(bank[:, t * P:(t + 1) * P], xin[:, t, c * P:(c + 1) * P], ident[:, :])
                return mm

            def l0_products(it, key):
                q = before_it(it)
                name, i = key[0], key[-1]
                bank = psum[FIRST_BANK[key]] if it is None else claim(pe, it, key)
                if name == "xT":
                    pe.wait_ge(x_in, q * 16 + 16)
                    mm = transposes(bank, i)
                if name == "down":
                    pe.wait_ge(xT_split, q * C + C)
                    for c in range(C):
                        mm = three(bank[:, :], [w[:, c, :] for w in wdown], [x[:, c, :] for x in xT], c == 0, c == C - 1)
                if name == "expert":
                    pe.wait_ge(expert_ready, q + 1)
                    pe.wait_ge(g_split, q + 1)
                    mm = three(bank[:, :], [w[:, :] for w in wexp], hT, True, True)
                if name == "up":
                    pe.wait_ge(e_split, q + 1)
                    mm = three(bank[:, :], [x[:, i * P:(i + 1) * P] for x in hT], [w[:, :] for w in wup], True, True)
                mm.then_inc(first_full if it is None else full_of(key), 1)

            pe.wait_ge(weights_split, 2)
            for key in FIRST:
                l0_products(None, key)
            pe.wait_ge(weights_split, len(WEIGHTS))
            pe.wait_ge(v_zeroed, 2)
            with pe.Fori(0, B) as it:
                pe.wait_ge(x1_ready, it * T + T)
                for c in range(C):
                    transposes(claim(pe, it, ("x1T", c)), c).then_inc(full_of(("x1T", c)), 1)
                pe.wait_ge(x1T_split, it * C + C)
                for name, w in (("q", wq), ("k", wk)):
                    for m in range(C):
                        bank = claim(pe, it, (name, m))
                        for c in range(C):
                            mm = three(bank[:, :], [p[:, c, m * P:(m + 1) * P] for p in w],
                                       [x[:, c, :] for x in xT], c == 0, c == C - 1)
                        mm.then_inc(full_of((name, m)), 1)
                for t in range(T):
                    bank = claim(pe, it, ("v", t))
                    for c in range(C):
                        mm = three(bank[:, :], [x[:, c, t * P:(t + 1) * P] for x in xT],
                                   [p[:, c, :] for p in wv], c == 0, c == C - 1)
                    mm.then_inc(full_of(("v", t)), 1)

                for c in range(C):
                    l0_products(it, ("xT", c))

                pe.wait_ge(mask_ready, it * 1 + 1)
                pe.wait_ge(qk_stacked, it * 384 + 384)
                for n in range(SLOTS_ALL):
                    if n < HT:
                        h, j = n // T, n % T
                        bank = claim(pe, it, ("S", h, j))
                        pe.matmul(bank[:, :], ident_bf[:, :], mask_add[:, j, :], start=True, stop=False)
                        pe.matmul(bank[:, :], q_st[0:96, h, j * P:(j + 1) * P], k_st[0:96, h, :],
                                  start=False, stop=True).then_inc(full_of(("S", h, j)), 1)
                    if n in PE_L0:
                        l0_products(it, PE_L0[n])
                    if 0 <= n - LAG_T < HT:
                        h, j = (n - LAG_T) // T, (n - LAG_T) % T
                        if j == 0:
                            pe.wait_ge(prob_ready, 1 + it * HT + T * (h + 1))
                        bank = claim(pe, it, ("T", h, j))
                        for t in range(T):
                            mm = pe.transpose(bank[:, t * P:(t + 1) * P], prob[:, h % 2, t, j * P:(j + 1) * P],
                                              ident[:, :])
                        mm.then_inc(full_of(("T", h, j)), 1)
                    if 0 <= n - LAG_PV < HT:
                        h, j = (n - LAG_PV) // T, (n - LAG_PV) % T
                        key = ("ctx", h // 4)
                        if h % 4 == 0 and j == 0:
                            claim(pe, it, key)
                            pe.wait_ge(v_split, 1 + it * T + T)
                        bank = psum[banks.place[key][0]]
                        pe.wait_ge(pT_split, 1 + it * HT + T * h + j + 1)
                        mm = three(bank[:, :], [v[:, j, h, :] for v in v_pad], [p[:, h % 2, j, :] for p in pT],
                                   h % 4 == 0 and j == 0, h % 4 == 3 and j == T - 1)
                        if j == T - 1:
                            mm.then_inc(pv_done, 1)
                    for g in range(G):
                        if n == turn_slot(g):
                            bank = claim(pe, it, ("R", g))
                            pe.wait_ge(rinv_ready, it * G + g + 1)
                            for t in range(T):
                                mm = pe.transpose(bank[:, t * P:(t + 1) * P], rinv_x[:, t, :], ident[:, :])
                            mm.then_inc(full_of(("R", g)), 1)
                for t in range(T):
                    bank = claim(pe, it, ("wo", t))
                    for c in range(C):
                        pe.wait_ge(ctx_split, 1 + it * G + c + 1)
                        mm = three(bank[:, :], [x[:, c, t * P:(t + 1) * P] for x in xT],
                                   [p[:, c, :] for p in wo], c == 0, c == C - 1)
                    mm.then_inc(full_of(("wo", t)), 1)

        @block.scalar
        def _(act):
            begin(act, "scalar")

            def l0_part(it, key):
                q = before_it(it)
                if key[0] == "xT":
                    bank = l0_tile(act, it, key)
                    act.activation(xT[0][:, key[1], :], bank[:, :], ACT.Copy).then_inc(x_hi, 1)
                if key[0] == "down":
                    bank = l0_tile(act, it, key)
                    act.activation(hid32[:, :], bank[:, :], ACT.Gelu, scale=1.0 / WS, bias=down_b[:, :])\
                        .then_inc(hid_ready, 1)
                if key[0] == "expert":
                    act.wait_ge(expert_ready, q + 1)
                    act.wait_ge(g_split, q + 1)
                    bank = l0_tile(act, it, key)
                    act.activation(hid32[:, :], bank[:, :], ACT.Identity, scale=1.0 / WS, bias=exp_bias[:, :])\
                        .then_inc(hid_ready, 1)

                if key[0] in ("scale0", "scale1"):
                    which, t = int(key[0] == "scale1"), key[1]
                    act.wait_ge(rstd_ready, q * 2 + which + 1)
                    act.activation(xin[:, t, :], xin[:, t, :], ACT.Identity, scale=rstd[:, t:t + 1],
                                   bias=shift[:, t:t + 1]).then_inc(scaled1 if which else scaled0, 1)

            def weight_hi(i):
                hi = WEIGHTS[i][1][0]
                act.wait_ge(raw_in[i % 2], 16 * (i // 2 + 1))
                act.activation(weight_view(hi), raw_view(i, hi), ACT.Copy, scale=WS).then_inc(weights_hi, 1)

            weight_hi(0)
            weight_hi(1)
            act.wait_ge(vec_in, 16 * len(VECS))
            for key in FIRST[:6]:
                l0_part(None, key)
            weight_hi(2)
            weight_hi(3)
            for t in range(T):
                l0_part(None, ("scale0", t))
            weight_hi(4)
            for t in range(T):
                l0_part(None, ("scale1", t))
            weight_hi(5)
            with act.Fori(0, B) as it:
                def copy_hi(key, dst, scale):
                    bank = arrived(act, it, key)
                    act.activation(dst, bank[:, :], ACT.Copy, scale=scale).then_inc(hi_done, 1)

                def to_f32(n, key, func, scale, bias_ap):
                    bank = arrived(act, it, key)
                    split, per, k = f32_split(n - 2 if n >= 2 else 10 + n)
                    act.wait_ge(split, base.get(split, 0) + it * per + (k if n >= 2 else 0))
                    dst = f32t[:, n % 2, :]
                    if bias_ap is None:
                        ins = act.activation(dst, bank[:, :], func, scale=scale)
                    else:
                        ins = act.activation(dst, bank[:, :], func, scale=scale, bias=bias_ap)
                    ins.then_inc(f32_ready, 1)

                for c in range(C):
                    copy_hi(("x1T", c), xT[0][:, c, :], 1.0)
                for m in range(C):
                    to_f32(m, ("q", m), ACT.Identity, 1.0 / (WS * math.sqrt(HD)), bq[:, m:m + 1])
                for m in range(C):
                    to_f32(C + m, ("k", m), ACT.Identity, 1.0 / WS, bk[:, m:m + 1])
                for t in range(T):
                    to_f32(2 * C + t, ("v", t), ACT.Copy, 1.0 / WS, None)
                for c in range(C):
                    l0_part(it, ("xT", c))
                for n in range(SLOTS_ALL):
                    if 0 <= n - LAG_T < HT:
                        h, j = (n - LAG_T) // T, (n - LAG_T) % T
                        if j == 0:
                            act.wait_ge(pv_done, 1 + it * H + max(0, h - 1))
                        copy_hi(("T", h, j), pT[0][:, h % 2, j, :], PS)
                    if n < HT:
                        h, j = n // T, n % T
                        act.wait_ge(scored, 1 + it * HT + n + 1)
                        act.activation(prob[:, h % 2, j, :], negs[:, j % NT, :], ACT.Exp, scale=-1.0,
                                       bias=nmax[:, h % 2, j:j + 1],
                                       accum_out=rsum[:, j, h:h + 1]).then_inc(prob_ready, 1)
                    if n in ACT_L0:
                        l0_part(it, ACT_L0[n])
                    for g in range(G):
                        if n == turn_slot(g) + 1:
                            bank = arrived(act, it, ("R", g))
                            act.wait_ge(ctx_ready, 1 + it * G + g)
                            act.wait_ge(e_split, it + 2)
                            act.activation(rinv_T[:, :], bank[:, :], ACT.Copy).then_inc(rinv_T_ready, 1)
                        if n == ctx_slot(g):
                            act.wait_ge(ctx_ready, 1 + it * G + g + 1)
                            act.activation(xT[0][:, g, :], ctx32[:, :], ACT.Identity, bias=bv[:, g:g + 1])\
                                .then_inc(ctx_hi, 1)
                for t in range(T):
                    act.wait_ge(x2_ready, 1 + it * T + t + 1)
                    act.dma_start(x2_dram[it, t * P:(t + 1) * P, :], x1[:, t, :]).then_inc(x2_out, 16)
            act.wait_ge(x2_out, 1 + B * 64)

        @block.vector
        def _(dve):
            links = [0]

            def chained(base):
                def link(ins):
                    links[0] += 1
                    ins.then_inc(chain, 1)
                    dve.wait_ge(chain, base + links[0])
                return link

            begin(dve, "vector")
            link = chained(0)
            dve.wait_ge(dom_in, 16)
            link(dve.tensor_copy(dom_f[:, :], dom[:, :]))
            link(dve.tensor_scalar(valid[:, :], dom_f[:, :], 0.0, None, ALU.is_ge))
            link(dve.tensor_scalar(invalid[:, :], dom_f[:, :], float(NE0), None, ALU.is_lt))
            link(dve.tensor_tensor(valid[:, :], valid[:, :], invalid[:, :], ALU.mult))
            link(dve.tensor_scalar(invalid[:, :], valid[:, :], -1.0, 1.0, ALU.mult, ALU.add))
            dve.tensor_scalar(dom_at[:, :], dom[0:1, :], 0, NE0 - 1, ALU.max, ALU.min).then_inc(dom_clipped, 1)

            def weight_lo(i):
                hi, lo = WEIGHTS[i][1]
                dve.wait_ge(weights_hi, i + 1)
                dve.scalar_tensor_tensor(out=weight_view(lo), in0=raw_view(i, hi), scalar=WS, in1=weight_view(hi),
                                         op0=ALU.mult, op1=ALU.subtract).then_inc(weights_split, 1)

            def diagonal(v, t):
                part = v[:, t, :, :]
                return bass.AP(tensor=part.tensor, offset=part.offset,
                               ap=[list(part.ap[0]), [4 * P, G], [P + HD, 4], [1, HD]])

            def l0_part(link, it, part):
                q = before_it(it)
                name, i = part[0], part[-1]
                col = slice(0, 1) if it is None else bass.ds((it + 1) % B, 1)
                if name == "expert_weights":
                    dve.wait_ge(expert_in, q * 32 + 32)
                    link(dve.tensor_scalar(exp_eff[:, :], exp_raw[:, :], valid[:, col], None, ALU.mult))
                    link(dve.scalar_tensor_tensor(out=exp_eff[:, :], in0=ident[:, :], scalar=invalid[:, col],
                                                  in1=exp_eff[:, :], op0=ALU.mult, op1=ALU.add))
                    link(dve.tensor_scalar(wexp[0][:, :], exp_eff[:, :], WS, None, ALU.mult))
                    link(dve.scalar_tensor_tensor(out=wexp[1][:, :], in0=exp_eff[:, :], scalar=WS, in1=wexp[0][:, :],
                                                  op0=ALU.mult, op1=ALU.subtract))
                    dve.scalar_tensor_tensor(out=exp_bias[:, :], in0=exp_vec[:, 0:1], scalar=valid[:, col],
                                             in1=exp_vec[:, 1:2], op0=ALU.mult, op1=ALU.add).then_inc(expert_ready, 1)
                if name == "xT":
                    bank = psum[FIRST_BANK[part] if it is None else banks.place[part][0]]
                    dve.wait_ge(x_hi, q * C + i + 1)
                    dve.tensor_tensor(xT[1][:, i, :], bank[:, :], xT[0][:, i, :], ALU.subtract).then_inc(xT_split, 1)
                if name in ("g", "e"):
                    dve.wait_ge(hid_ready, q * 2 + (1 if name == "g" else 2))
                    link(dve.tensor_copy(hT[0], hid32[:, :]))
                    dve.tensor_tensor(hT[1], hid32[:, :], hT[0], ALU.subtract)\
                        .then_inc(g_split if name == "g" else e_split, 1)
                if name == "y":
                    bank = l0_tile(dve, it, ("up", i))
                    dve.wait_ge(xb_ready, q * T + i + 1)
                    dve.scalar_tensor_tensor(out=xin[:, i, :], in0=bank[:, :], scalar=1.0 / WS, in1=xin[:, i, :],
                                             op0=ALU.mult, op1=ALU.add).then_inc(y_ready, 1)
                if name in ("stats0", "stats1"):
                    dve.wait_ge(*((y_ready, q * T + i + 1) if name == "stats0" else (ln0_ready, q * T + i + 1)))
                    link(dve.bn_stats(stats[:, i, :], xin[:, i, :]))
                    dve.sem_inc(carrier, 1)
                    link(dve.bn_aggr(mv[:, i, :], stats[:, i, :]))
                if name == "rstd":
                    link(dve.tensor_scalar(var[:, :], mv[:, :, 1], 1e-5, None, ALU.add))
                    rsqrt_steps(dve, link, var[:, :], rstd[:, :], newt[:, :], rstd[:, :].bitcast(I32),
                                var[:, :].bitcast(I32))
                    dve.scalar_tensor_tensor(out=shift[:, :], in0=mv[:, :, 0], scalar=-1.0, in1=rstd[:, :],
                                             op0=ALU.mult, op1=ALU.mult).then_inc(rstd_ready, 1)

            dve.wait_ge(ident_set, 2)
            dve.wait_ge(vec_in, 16 * len(VECS))
            for i in range(2):
                weight_lo(i)
            todo = list(range(2, len(WEIGHTS)))
            l0_part(link, None, ("expert_weights",))
            for c in range(C):
                l0_part(link, None, ("xT", c))
            for part in DVE_L0.values():
                l0_part(link, None, part)
                if part == ("rstd",):
                    weight_lo(todo.pop(0))
                    weight_lo(todo.pop(0))
            link(dve.tensor_scalar(bq[:, :], bq[:, :], 1.0 / math.sqrt(HD), None, ALU.mult))
            dve.wait_ge(v_zeroed, 2)
            before = links[0]

            with dve.Fori(0, B) as it:
                links[0] = 0
                link = chained(it * LINKS_A + before)

                def lo_of(key, k, hi, lo, signal, scale=None):
                    bank = psum[banks.place[key][0]]
                    dve.wait_ge(hi_done, it * (C + H * T) + k + 1)
                    if scale is None:
                        ins = dve.tensor_tensor(lo, bank[:, :], hi, ALU.subtract)
                    else:
                        ins = dve.scalar_tensor_tensor(out=lo, in0=bank[:, :], scalar=scale, in1=hi,
                                                       op0=ALU.mult, op1=ALU.subtract)
                    ins.then_inc(signal, 1)

                def split_f32(k, hi, lo, signal):
                    dve.wait_ge(f32_ready, it * 12 + k + 1)
                    src = f32t[:, k % 2, :]
                    link(dve.tensor_copy(hi, src))
                    dve.tensor_tensor(lo, src, hi, ALU.subtract).then_inc(signal, 1)

                dve.wait_ge(mask_in, it * 16 + 16)
                dve.tensor_scalar(mask_add[:, :, :], mask_raw[:, :, :], NEG, None, ALU.mult).then_inc(mask_ready, 1)
                for c in range(C):
                    lo_of(("x1T", c), c, xT[0][:, c, :], xT[1][:, c, :], x1T_split)
                for m in range(C):
                    split_f32(m, qT[0][:, m, :], qT[1][:, m, :], qk_split)
                l0_part(link, it, ("expert_weights",))
                for m in range(C):
                    split_f32(C + m, kT[0][:, m, :], kT[1][:, m, :], qk_split)
                for t in range(T):
                    dve.wait_ge(f32_ready, it * 12 + 2 * C + t + 1)
                    src = f32t[:, t % 2, :].rearrange("p (g i d) -> p g i d", i=4, d=HD)
                    hi, lo = (diagonal(v, t) for v in v_pad)
                    link(dve.tensor_copy(hi, src))
                    dve.tensor_tensor(lo, src, hi, ALU.subtract).then_inc(v_split, 1)
                for c in range(C):
                    l0_part(link, it, ("xT", c))
                dve.wait_ge(v_split, 1 + it * T + T)

                for n in range(SLOTS_ALL):
                    for g in range(G):
                        if n == rinv_slot(g):
                            dve.wait_ge(prob_ready, 1 + it * HT + 4 * T * (g + 1))
                            link(dve.reciprocal(rinv[:, :, :], rsum[:, :, 4 * g:4 * g + 4]))
                            dve.tensor_copy(rinv_x[:, :, :].rearrange("p t (i d) -> p t i d", d=HD),
                                            rinv[:, :, :].unsqueeze(3).to_broadcast([P, T, 4, HD]))\
                                .then_inc(rinv_ready, 1)
                        if n == ctx_slot(g):
                            bank = psum[banks.place["ctx", g][0]]
                            dve.wait_ge(pv_done, 1 + it * H + 4 * g + 4)
                            dve.wait_ge(rinv_T_ready, it * G + g + 1)
                            dve.wait_ge(ctx_split, 1 + it * G + g)
                            dve.scalar_tensor_tensor(out=ctx32[:, :], in0=bank[:, :], scalar=1.0 / PS,
                                                     in1=rinv_T[:, :], op0=ALU.mult, op1=ALU.mult)\
                                .then_inc(ctx_ready, 1)
                        if n == ctx_slot(g) + 1:
                            dve.wait_ge(ctx_hi, it * G + g + 1)
                            dve.wait_ge(ctx_ready, 1 + it * G + g + 1)
                            dve.scalar_tensor_tensor(out=xT[1][:, g, :], in0=ctx32[:, :], scalar=bv[:, g:g + 1],
                                                     in1=xT[0][:, g, :], op0=ALU.add, op1=ALU.subtract)\
                                .then_inc(ctx_split, 1)
                    if n < HT:
                        h, j = n // T, n % T
                        half = n // 2
                        bank = arrived(dve, it, ("S", h, j))
                        if j % 2 == 0:
                            dve.wait_ge(bias_in[half % NB], (it * (2 * H // NB) + half // NB + 1) * 16)
                        dve.wait_ge(prob_ready, 1 + it * HT + max(0, n - NT + 1))
                        dve.sem_inc(carrier, 1)
                        dve.tensor_tensor_reduce(negs[:, j % NT, :], bank[:, :], bias[:, half % NB, j % 2, :],
                                                 -1.0, 3.0e38, ALU.add, ALU.min, nmax[:, h % 2, j:j + 1])\
                            .then_inc(scored, 1)
                    if n in DVE_L0:
                        l0_part(link, it, DVE_L0[n])
                    if 0 <= n - LAG_T < HT:
                        h, j = (n - LAG_T) // T, (n - LAG_T) % T
                        lo_of(("T", h, j), C + n - LAG_T, pT[0][:, h % 2, j, :], pT[1][:, h % 2, j, :], pT_split, PS)
                for t in range(T):
                    bank = arrived(dve, it, ("wo", t))
                    dve.wait_ge(x1b_ready, it * T + t + 1)
                    dve.scalar_tensor_tensor(out=x1[:, t, :], in0=bank[:, :], scalar=1.0 / WS, in1=x1[:, t, :],
                                             op0=ALU.mult, op1=ALU.add).then_inc(x2_ready, 1)
            assert links[0] == LINKS_A, [0, links[0]]


STEPS = 2 * NF
LAG_DOWN = 2
NW = 6
ALPHA = [3, 5, 7, 9]
STENCIL = {10: 0, 12: 1}
BETA = [11, 13, 15, 17]
SUM = [11, 13, NF, 17]
RELU = [11, 13, NF, 17]
CHUNK = {k: (2 + 2 * k if k < NW else NF + k - 3) for k in range(NF)}
NORM2 = 2 * NF - 9


def ffn_pass(nc, a, x2_dram, out):
    order, ring = [], 0

    def in_ring(key):
        nonlocal ring
        order.append((key, 4 + ring % 4))
        ring += 1

    for n in range(STEPS):
        if n == NF:
            order += [(("x3T", c), c) for c in range(C)]
            in_ring(("L3", 2))
            in_ring(("L3", 3))
        in_ring(("up", n))
        if n in STENCIL:
            in_ring(("L3", STENCIL[n]))
    for c in range(C):
        in_ring(("h2T", c))
    banks = Banks(order)

    with ExitStack() as ctx:
        def sb(name, shape, dt):
            return ctx.enter_context(nc.sbuf_tensor(name, shape, dt))

        def sem(name):
            return ctx.enter_context(nc.semaphore(name))

        w1 = [sb(f"w1_{h}", [P, C, FF], F16) for h in ("hi", "lo")]
        w2 = [sb(f"w2_{h}", [P, NF, D], F16) for h in ("hi", "lo")]
        wl = [sb(f"wl_{h}", [P, NW, 2 * D], F16) for h in ("hi", "lo")]
        raw = sb("raw2", [P, 2, 2 * D], F32)
        ident = sb("ident2", [P, P], F32)
        dmat = sb("dmat", [P, 10, P], F16)
        b1 = sb("b1", [P, NF], F32)
        bi = sb("bi", [P, NF], F32)
        dt = sb("dt", [P, B], F32)
        idx = sb("idx", [1, B], I32)
        g2, beta2, b2 = (sb(n, [P, D], F32) for n in ("g2", "beta2", "b2"))
        l2_rows = sb("l2_rows", [P, 3, D], F32)
        x2n = sb("x2n", [P, T, D], F32)
        x2 = sb("x2", [P, T, D], F32)
        h2 = sb("h2", [P, T, D], F32)
        f = sb("f", [P, T, D], F32)
        xT = [sb(f"x3T_{h}", [P, C, S], F16) for h in ("hi", "lo")]
        g32 = sb("g32", [P, 2, S], F32)
        gT = [sb(f"g2T_{h}", [P, 4, S], F16) for h in ("hi", "lo")]
        grid = sb("grid", [P, 3, D], F32)
        prod = sb("prod", [P, 4, D], F32)
        tmp = sb("tmp", [P, 2, D], F32)
        vsp = [sb(f"vsp_{h}", [P, T, D], F16) for h in ("hi", "lo")]
        msp = [sb(f"msp_{h}", [P, T, D], F16) for h in ("hi", "lo")]
        outt = sb("outt", [P, 2, D], F32)
        edge = sb("edge", [P, 4], F32)
        stats = sb("stats2", [P, T, 6], F32)
        mv = sb("mv2", [P, T, 2], F32)
        var = sb("var2", [P, T], F32)
        rstd = sb("rstd2", [P, T], F32)
        newt = sb("newt2", [P, T], F32)

        psum = [ctx.enter_context(nc.psum_tensor(f"ffn_bank{i}", [P, S], F32)) for i in range(8)]
        full = [sem(f"ffn_bank{i}_full") for i in range(8)]

        vec_in = sem("ffn_vec_in")
        idx_in = sem("idx_in")
        idx_clipped = sem("idx_clipped")
        dmat_in = sem("dmat_in")
        w_raw_in = [sem(f"w_raw{i}_in") for i in range(6)]
        w_hi = sem("w_hi")
        w_split = sem("w_split")
        ident_set = sem("ffn_ident_set")
        zeroed = sem("zeroed")
        x2_in = sem("x2_in")
        rows_in = sem("rows_in")
        chunk_in = [sem(f"chunk{i}_in") for i in range(2)]
        chunk_hi = sem("chunk_hi")
        chunk_split = sem("chunk_split")
        alpha_in = sem("alpha_grids_in")
        beta_in = sem("beta_grids_in")
        hi_done = sem("ffn_hi_done")
        first_full = sem("first_h2T_full")
        h2T_split = sem("h2T_split")
        x3T_split = sem("x3T_split")
        gelu_ready = sem("gelu_ready")
        g_split = sem("ffn_g_split")
        down_done = sem("down_done")
        acc_full = sem("acc_full")
        x3_ready = sem("x3_ready")
        x3b_ready = sem("x3b_ready")
        r_ready = sem("r_ready")
        x2b_ready = sem("x2b_ready")
        scaled2 = sem("scaled2")
        h2_ready = sem("h2_ready")
        scaled3 = sem("scaled3")
        f_ready = sem("f_ready")
        alpha_prod = sem("alpha_prod")
        alpha_done = sem("alpha_done")
        beta_prod = sem("beta_prod")
        y_done = sem("y_part_done")
        sum_ready = sem("stencil_sum_ready")
        step_ready = sem("step_ready")
        out_ready = sem("out_ready")
        out_stored = [sem(f"out{i}_stored") for i in range(2)]
        chain = sem("ffn_dve_chain")
        carrier = sem("ffn_wait_carrier")

        block = ctx.enter_context(nc.Block())

        BEGUN = {"vector": (sum_ready, chunk_split, y_done, r_ready, g_split),
                 "gpsimd": (beta_prod,), "scalar": (gelu_ready, out_ready, *out_stored)}
        base = {s: 1 for sems in BEGUN.values() for s in sems}
        base[h2T_split] = C

        def begin(eng, name):
            for s in BEGUN[name]:
                eng.sem_inc(s, 1)

        def claim(pe, it, key):
            bank, _, last = banks.place[key]
            k = last[1]
            signal, per = {"h2T": (h2T_split, C), "x3T": (x3T_split, C), "up": (gelu_ready, STEPS),
                           "L3": (sum_ready, T)}[last[0]]
            pe.wait_ge(signal, base.get(signal, 0) + it * per + (0 if banks.first[key] else k + 1))
            return psum[bank]

        def arrived(eng, it, key):
            bank, before, _ = banks.place[key]
            eng.wait_ge(full[bank], it * banks.uses[bank] + before + 1)
            return psum[bank]

        def full_of(key):
            return full[banks.place[key][0]]

        def downs(n):
            return n + 1 - n // NF

        COLS = [(b1[:, :], a["b1"]), (dt[:, :], a["dt"].partition_broadcast(P)),
                (g2[:, :], a["g2"].partition_broadcast(P)), (beta2[:, :], a["beta2"].partition_broadcast(P)),
                (b2[:, :], a["b2"].partition_broadcast(P))]
        PIECES = []
        for c in range(C):
            for half in range(2):
                cols = slice(half * 1024, (half + 1) * 1024)
                PIECES.append((a["W1"][c * P:(c + 1) * P, cols], w1[0][:, c, cols], w1[1][:, c, cols]))
        for k in range(0, NF, 2):
            src = a["W2"][k * P:(k + 2) * P, :].rearrange("(k p) n -> p k n", p=P)
            PIECES.append((src, w2[0][:, k:k + 2, :], w2[1][:, k:k + 2, :]))

        RAWS = [raw[:, 0, :], raw[:, 1, :]]
        RAWS += [v.rearrange("p k d -> p (k d)") for v in (prod[:, 0:2, :], prod[:, 2:4, :], tmp[:, :, :], outt[:, :, :])]
        NR = len(RAWS)

        def piece_raw(i):
            v = RAWS[i % NR]
            return v if i < 2 * C else v.rearrange("p (k n) -> p k n", k=2)

        def stencil_load(sp, it, kind, t):
            rows = slice(t * P, (t + 1) * P)
            if kind == "alpha":
                if t:
                    sp.wait_ge(alpha_prod, it * 12 + 3 * t)
                else:
                    sp.wait_ge(beta_prod, 1 + it * 16)
                for i, g in enumerate((0, 2, 4)):
                    sp.dma_start(grid[:, i, :], a["grids"][g, rows, :]).then_inc(alpha_in, 16)
            else:
                if t:
                    sp.wait_ge(beta_prod, 1 + it * 16 + 4 * t)
                else:
                    sp.wait_ge(alpha_prod, it * 12 + 12)
                for i, g in enumerate((1, 3)):
                    sp.dma_start(grid[:, i, :], a["grids"][g, rows, :]).then_inc(beta_in, 16)

        @block.sync
        def _(sp):
            sp.dma_start(idx[:, :], a["idx2"].rearrange("(o b) -> o b", o=1)).then_inc(idx_in, 16)
            sp.dma_start(x2n[:, :, :], x2_dram[0].rearrange("(t p) d -> p t d", p=P)).then_inc(x2_in, 16)
            for dst, src in COLS:
                sp.dma_start(dst, src).then_inc(vec_in, 16)
            for i, (src, _, _) in enumerate(PIECES):
                if i >= NR:
                    sp.wait_ge(w_split, i - NR + 1)
                sp.dma_start(piece_raw(i), src).then_inc(w_raw_in[i % NR], 16)
            sp.dma_start(dmat[:, :, :], a["dmat"]).then_inc(dmat_in, 16)
            sp.wait_ge(w_split, len(PIECES))
            sp.wait_ge(idx_clipped, 1)
            with sp.Fori(0, B) as it:
                e = sp.value_load(idx[0:1, bass.ds(it, 1)], min_val=0, max_val=NE2 - 1)

                def load_chunk(k):
                    sp.wait_ge(chunk_split, 1 + it * NF + max(0, k - 1))
                    sp.dma_start(raw[:, k % 2, :], a["W_l2"][e, k]).then_inc(chunk_in[k % 2], 16)

                def load_rows():
                    sp.wait_ge(f_ready, it * T + T)
                    sp.dma_start(bi[:, :], a["bi"][e]).then_inc(rows_in, 16)
                    sp.dma_start(l2_rows[:, :, :], a["rows2"][e].partition_broadcast(P)).then_inc(rows_in, 16)

                def load_next_x2():
                    sp.wait_ge(x2b_ready, it * T + T)
                    nxt = (it + 1) % B
                    sp.dma_start(x2n[:, :, :], x2_dram[nxt].rearrange("(t p) d -> p t d", p=P)).then_inc(x2_in, 16)

                loads = [(CHUNK[k - 2] if k >= 2 else -1, 0, load_chunk, (k,)) for k in range(NF)]
                loads += [(ALPHA[t - 1] if t else -1, 1, stencil_load, (sp, it, "alpha", t)) for t in range(T)]
                loads += [(BETA[t - 1] if t else ALPHA[-1], 1, stencil_load, (sp, it, "beta", t)) for t in range(T)]
                loads += [(1, 2, load_rows, ()), (1, 3, load_next_x2, ())]
                for _, _, load, args in sorted(loads, key=lambda x: x[:2]):
                    load(*args)
            for t in range(T):
                stencil_load(sp, B, "alpha", t)
            for t in range(T):
                stencil_load(sp, B, "beta", t)

        def add_beta3(pool, it):
            for t in range(T):
                pool.wait_ge(scaled3, it * T + t + 1)
                pool.tensor_tensor(f[:, t, :], f[:, t, :], l2_rows[:, 2, :], ALU.add).then_inc(f_ready, 1)

        def alpha_products(pool, it, t):
            pool.wait_ge(f_ready, it * T + t + 1)
            pool.wait_ge(alpha_in, (it * T + t + 1) * 48)
            if t:
                pool.wait_ge(alpha_done, it * T + t)
            else:
                pool.wait_ge(sum_ready, 1 + it * T)
            for i in (2, 0, 1):
                pool.tensor_tensor(prod[:, i, :], grid[:, i, :], f[:, t, :], ALU.mult).then_inc(alpha_prod, 1)

        def beta_products(pool, it, t):
            pool.wait_ge(beta_in, (it * T + t + 1) * 32)
            pool.wait_ge(alpha_done, it * T + T)
            pool.wait_ge(y_done, 1 + it * T + t)
            for i in range(2):
                pool.tensor_tensor(prod[:, i, :], grid[:, i, :], f[:, t, :], ALU.mult).then_inc(beta_prod, 1)
            pool.wait_ge(beta_prod, 1 + it * 16 + 4 * t + 2)
            pool.tensor_tensor(prod[:, 2, :], prod[:, 1, :], prod[:, 0, :], ALU.subtract).then_inc(beta_prod, 1)
            pool.tensor_tensor(prod[:, 3, :], prod[:, 1, :], prod[:, 0, :], ALU.add).then_inc(beta_prod, 1)

        def move_x2(pool, count, t):
            pool.tensor_tensor(x2[:, t, :], x2n[:, t, :], b2[:, :], ALU.add).then_inc(x2b_ready, 1)

        @block.gpsimd
        def _(pool):
            begin(pool, "gpsimd")
            pool.memset(ident[:, :], 0.0).then_inc(ident_set, 1)
            pool.wait_ge(ident_set, 1)
            pool.affine_select(out=ident[:, :], in_=ident[:, :], compare_op=ALU.not_equal, fill=1.0, base=0,
                               pattern=[[-1, P]], channel_multiplier=1).then_inc(ident_set, 1)
            pool.memset(f[:, :, :], 0.0).then_inc(zeroed, 1)
            pool.memset(l2_rows[:, :, :], 0.0).then_inc(zeroed, 1)
            pool.wait_ge(vec_in, 16 * len(COLS))
            pool.wait_ge(x2_in, 16)
            pool.wait_ge(zeroed, 2)
            for t in range(T):
                move_x2(pool, 0, t)
            for t in range(T):
                pool.wait_ge(scaled2, t + 1)
                pool.tensor_tensor(h2[:, t, :], h2[:, t, :], beta2[:, :], ALU.add).then_inc(h2_ready, 1)
            with pool.Fori(0, B) as it:
                add_beta3(pool, it)
                for t in range(T):
                    alpha_products(pool, it, t)
                for t in range(T):
                    beta_products(pool, it, t)
                arrived(pool, it, ("x3T", C - 1))
                pool.wait_ge(rows_in, it * 32 + 32)
                for t in range(T):
                    pool.tensor_tensor(x2[:, t, :], x2[:, t, :], l2_rows[:, 0, :], ALU.add).then_inc(x3b_ready, 1)
                for t in range(T):
                    pool.wait_ge(scaled2, it * T + T + t + 1)
                    pool.tensor_tensor(h2[:, t, :], h2[:, t, :], beta2[:, :], ALU.add).then_inc(h2_ready, 1)
                for t in range(T):
                    pool.wait_ge(r_ready, 1 + it * T + t + 1)
                    move_x2(pool, it, t)
            add_beta3(pool, B)
            for t in range(T):
                alpha_products(pool, B, t)
            for t in range(T):
                beta_products(pool, B, t)

        def stencil(pe, bank, t):
            terms = []
            for m, parts in ((0, vsp), (5, msp)):
                diag = m + (0 if t == 0 else 2 if t == T - 1 else 1)
                for blk, tt in ((diag, t), (m + 3, t - 1), (m + 4, t + 1)):
                    if 0 <= tt < T:
                        terms += [(blk, part[:, tt, :]) for part in parts]
            for i, (blk, x) in enumerate(terms):
                mm = pe.matmul(bank[:, :], dmat[:, blk, :], x, start=(i == 0), stop=(i == len(terms) - 1))
            return mm

        @block.tensor
        def _(pe):
            def three(out, w, x, first, last):
                pe.matmul(out, w[0], x[0], start=first, stop=False)
                pe.matmul(out, w[0], x[1], start=False, stop=False)
                return pe.matmul(out, w[1], x[0], start=False, stop=last)

            pe.wait_ge(ident_set, 2)
            pe.wait_ge(w_split, len(PIECES))
            pe.wait_ge(dmat_in, 16)
            def h2_transposes(bank, c):
                for t in range(T):
                    mm = pe.transpose(bank[:, t * P:(t + 1) * P], h2[:, t, c * P:(c + 1) * P], ident[:, :])
                return mm

            pe.wait_ge(h2_ready, T)
            for c in range(C):
                h2_transposes(psum[c], c).then_inc(first_full, 1)
            with pe.Fori(0, B) as it:
                def up(n):
                    bank = claim(pe, it, ("up", n))
                    k = n % NF
                    if n >= NF:
                        pe.wait_ge(chunk_split, 1 + it * NF + k + 1)
                    for c in range(C):
                        if n % NF == 0:
                            if n:
                                pe.wait_ge(x3T_split, it * C + c + 1)
                            else:
                                pe.wait_ge(h2T_split, it * C + C)
                        w = [x[:, c, k * P:(k + 1) * P] for x in w1] if n < NF else \
                            [x[:, k % NW, c * P:(c + 1) * P] for x in wl]
                        mm = three(bank[:, :], w, [x[:, c, :] for x in xT], c == 0, c == C - 1)
                    mm.then_inc(full_of(("up", n)), 1)

                def down(n):
                    k = n % NF
                    pe.wait_ge(g_split, 1 + it * STEPS + n + 1)
                    w = [x[:, k, :] for x in w2] if n < NF else [x[:, k % NW, D:2 * D] for x in wl]
                    for t in range(T):
                        if n == 0 and t == 0:
                            pe.wait_ge(r_ready, 1 + it * T)
                        mm = three(psum[t][:, :], [x[:, n % 4, t * P:(t + 1) * P] for x in gT], w, k == 0, k == NF - 1)
                        if k == NF - 1:
                            mm.then_inc(acc_full, 1)
                    if k < NF - 1:
                        mm.then_inc(down_done, 1)

                def run_stencil(t):
                    bank = claim(pe, it, ("L3", t))
                    pe.wait_ge(alpha_done, it * T + T)
                    stencil(pe, bank, t).then_inc(full_of(("L3", t)), 1)

                for half in range(2):
                    if half:
                        run_stencil(2)
                        for t in range(T):
                            pe.wait_ge(x3_ready, it * T + T)
                            for c in range(C):
                                mm = pe.transpose(psum[c][:, t * P:(t + 1) * P], x2[:, t, c * P:(c + 1) * P], ident[:, :])
                                if t == T - 1:
                                    mm.then_inc(full_of(("x3T", c)), 1)
                        run_stencil(3)
                    for n in range(half * NF, half * NF + NF):
                        up(n)
                        if n - LAG_DOWN >= half * NF:
                            down(n - LAG_DOWN)
                        if n in STENCIL:
                            run_stencil(STENCIL[n])
                    if half:
                        pe.wait_ge(h2_ready, it * T + 2 * T)
                        for c in range(C):
                            h2_transposes(claim(pe, it, ("h2T", c)), c).then_inc(full_of(("h2T", c)), 1)
                    for n in range(half * NF + NF - LAG_DOWN, half * NF + NF):
                        down(n)
            pe.wait_ge(alpha_done, B * T + T)
            pe.wait_ge(r_ready, 1 + B * T)
            for t in range(T):
                stencil(pe, psum[t], t).then_inc(full[t], 1)

        def relu_store(act, it, row, t):
            act.wait_ge(step_ready, it * T + t + 1)
            act.wait_ge(out_stored[t % 2], 1 + (it * (T // 2) + t // 2) * 16)
            act.activation(outt[:, t % 2, :], tmp[:, 1, :], ACT.Relu).then_inc(out_ready, 1)
            act.wait_ge(out_ready, 1 + it * T + t + 1)
            act.dma_start(out[row, t * P:(t + 1) * P, :], outt[:, t % 2, :]).then_inc(out_stored[t % 2], 16)

        @block.scalar
        def _(act):
            begin(act, "scalar")
            act.wait_ge(vec_in, 16 * len(COLS))
            for i, (_, hi, _) in enumerate(PIECES):
                act.wait_ge(w_raw_in[i % NR], 16 * (i // NR + 1))
                act.activation(hi, piece_raw(i), ACT.Copy, scale=WS).then_inc(w_hi, 1)
            for c in range(C):
                act.wait_ge(first_full, c + 1)
                act.activation(xT[0][:, c, :], psum[c][:, :], ACT.Copy).then_inc(hi_done, 1)
            with act.Fori(0, B) as it:
                prev = (it + (B - 1)) % B

                def copy_hi(key, c):
                    bank = arrived(act, it, key)
                    act.activation(xT[0][:, c, :], bank[:, :], ACT.Copy).then_inc(hi_done, 1)

                for n in range(STEPS):
                    if n == NF:
                        for c in range(C):
                            copy_hi(("x3T", c), c)
                        act.wait_ge(rows_in, it * 32 + 32)
                    bank = arrived(act, it, ("up", n))
                    act.wait_ge(g_split, 1 + it * STEPS + max(0, n - 1))
                    func, vec = (ACT.Gelu_apprx_sigmoid, b1) if n < NF else (ACT.Gelu, bi)
                    act.activation(g32[:, n % 2, :], bank[:, :], func, scale=1.0 / WS,
                                   bias=vec[:, n % NF:n % NF + 1]).then_inc(gelu_ready, 1)
                    for k in range(NF):
                        if CHUNK[k] == n:
                            act.wait_ge(chunk_in[k % 2], (it * (NF // 2) + k // 2 + 1) * 16)
                            if k >= NW:
                                act.wait_ge(down_done, it * (STEPS - 2) + downs(NF + k - NW))
                            act.activation(wl[0][:, k % NW, :], raw[:, k % 2, :], ACT.Copy, scale=WS)\
                                .then_inc(chunk_hi, 1)
                    if n in RELU:
                        relu_store(act, it, prev, RELU.index(n))
                for c in range(C):
                    copy_hi(("h2T", c), c)
            for t in range(T):
                relu_store(act, B, B - 1, t)
            for stored in out_stored:
                act.wait_ge(stored, 1 + (B + 1) * (T // 2) * 16)

        @block.vector
        def _(dve):
            links = [0]

            def chained(base):
                def link(ins):
                    links[0] += 1
                    ins.then_inc(chain, 1)
                    dve.wait_ge(chain, base + links[0])
                return link

            def norm_stats(link, src, t):
                link(dve.bn_stats(stats[:, t, :], src[:, t, :]))
                dve.sem_inc(carrier, 1)
                link(dve.bn_aggr(mv[:, t, :], stats[:, t, :]))

            def norm_rstd(link, eps):
                link(dve.tensor_scalar(var[:, :], mv[:, :, 1], eps, None, ALU.add))
                rsqrt_steps(dve, link, var[:, :], rstd[:, :], newt[:, :], rstd[:, :].bitcast(I32),
                            var[:, :].bitcast(I32))

            def norm_scale(link, dst, src, gain, t, signal):
                link(dve.tensor_scalar(dst[:, t, :], src[:, t, :], mv[:, t, 0:1], rstd[:, t:t + 1],
                                       ALU.subtract, ALU.mult))
                dve.tensor_tensor(dst[:, t, :], dst[:, t, :], gain, ALU.mult).then_inc(signal, 1)

            def norm3(link, it, part):
                if part == 0:
                    for t in range(T):
                        norm_stats(link, f, t)
                else:
                    if part == 1:
                        norm_rstd(link, 1e-12)
                    for t in (2 * part - 2, 2 * part - 1):
                        norm_scale(link, f, f, l2_rows[:, 1, :], t, scaled3)

            def alpha(link, it, t):
                dve.wait_ge(alpha_prod, it * 12 + 3 * t + 3)
                m0, m2, m1 = prod[:, 0, :], prod[:, 1, :], prod[:, 2, :]
                w = tmp[:, 0, :]
                link(dve.tensor_tensor(w[:, 1:D - 1], m1[:, 2:D], m1[:, 0:D - 2], ALU.subtract))
                ends = [m1[:, k:D - k:D - 1 - 2 * k] for k in range(3)]
                we = w[:, 0:D:D - 1]
                link(dve.tensor_scalar(we, ends[0], -3.0, None, ALU.mult))
                link(dve.scalar_tensor_tensor(out=we, in0=ends[1], scalar=4.0, in1=we, op0=ALU.mult, op1=ALU.add))
                link(dve.scalar_tensor_tensor(out=we, in0=ends[2], scalar=-1.0, in1=we, op0=ALU.mult, op1=ALU.add))
                link(dve.tensor_scalar(w[:, D - 1:D], w[:, D - 1:D], -1.0, None, ALU.mult))
                link(dve.scalar_tensor_tensor(out=w, in0=w, scalar=0.5, in1=m0, op0=ALU.mult, op1=ALU.subtract))
                link(dve.tensor_copy(vsp[0][:, t, :], w))
                dve.tensor_tensor(vsp[1][:, t, :], w, vsp[0][:, t, :], ALU.subtract)
                link(dve.tensor_copy(msp[0][:, t, :], m2))
                dve.tensor_tensor(msp[1][:, t, :], m2, msp[0][:, t, :], ALU.subtract).then_inc(alpha_done, 1)

            def beta(link, it, t):
                dve.wait_ge(beta_prod, 1 + it * 16 + 4 * t + 4)
                dve.wait_ge(alpha_done, it * T + T)
                pa, pb, less, plus = (prod[:, i, :] for i in range(4))
                s = tmp[:, 0, :]
                link(dve.tensor_tensor(s[:, 1:D - 1], less[:, 2:D], plus[:, 0:D - 2], ALU.add))
                link(dve.scalar_tensor_tensor(out=s[:, 1:D - 1], in0=s[:, 1:D - 1], scalar=0.5, in1=pb[:, 1:D - 1],
                                              op0=ALU.mult, op1=ALU.subtract))
                ea = [pa[:, k:D - k:D - 1 - 2 * k] for k in range(3)]
                eb = [pb[:, k:D - k:D - 1 - 2 * k] for k in range(4)]
                sa, sbb = edge[:, 0:2], edge[:, 2:4]
                link(dve.tensor_scalar(sa, ea[0], 1.5, None, ALU.mult))
                link(dve.scalar_tensor_tensor(out=sa, in0=ea[1], scalar=-2.0, in1=sa, op0=ALU.mult, op1=ALU.add))
                link(dve.scalar_tensor_tensor(out=sa, in0=ea[2], scalar=0.5, in1=sa, op0=ALU.mult, op1=ALU.add))
                link(dve.scalar_tensor_tensor(out=sbb, in0=eb[1], scalar=-2.5, in1=eb[0], op0=ALU.mult, op1=ALU.add))
                link(dve.scalar_tensor_tensor(out=sbb, in0=eb[2], scalar=2.0, in1=sbb, op0=ALU.mult, op1=ALU.add))
                link(dve.scalar_tensor_tensor(out=sbb, in0=eb[3], scalar=-0.5, in1=sbb, op0=ALU.mult, op1=ALU.add))
                link(dve.tensor_tensor(s[:, 0:1], sbb[:, 0:1], sa[:, 0:1], ALU.add))
                dve.tensor_tensor(s[:, D - 1:D], sbb[:, 1:2], sa[:, 1:2], ALU.subtract).then_inc(y_done, 1)

            def total(it, row, t, bank):
                s = tmp[:, 0, :]
                dve.wait_ge(y_done, 1 + it * T + t + 1)
                if bank is None:
                    bank = arrived(dve, it, ("L3", t))
                else:
                    dve.wait_ge(full[t], B + 1)
                dve.wait_ge(out_ready, 1 + it * T + t)
                dve.tensor_tensor(tmp[:, 1, :], bank[:, :], s, ALU.add).then_inc(sum_ready, 1)
                dve.wait_ge(sum_ready, 1 + it * T + t + 1)
                dve.scalar_tensor_tensor(out=tmp[:, 1, :], in0=tmp[:, 1, :], scalar=row, in1=f[:, t, :],
                                         op0=ALU.mult, op1=ALU.add).then_inc(step_ready, 1)

            begin(dve, "vector")
            link = chained(0)
            dve.wait_ge(idx_in, 16)
            dve.tensor_scalar(idx[:, :], idx[:, :], 0, NE2 - 1, ALU.max, ALU.min).then_inc(idx_clipped, 1)
            dve.wait_ge(x2_in, 16)
            dve.wait_ge(vec_in, 16 * len(COLS))
            dve.wait_ge(zeroed, 2)
            for t in range(T):
                norm_stats(link, x2n, t)
            norm_rstd(link, 1e-5)
            for t in range(T):
                norm_scale(link, h2, x2n, g2[:, :], t, scaled2)
            for i, (_, hi, lo) in enumerate(PIECES):
                dve.wait_ge(w_hi, i + 1)
                dve.scalar_tensor_tensor(out=lo, in0=piece_raw(i), scalar=WS, in1=hi,
                                         op0=ALU.mult, op1=ALU.subtract).then_inc(w_split, 1)
            for c in range(C):
                dve.wait_ge(hi_done, c + 1)
                dve.tensor_tensor(xT[1][:, c, :], psum[c][:, :], xT[0][:, c, :], ALU.subtract).then_inc(h2T_split, 1)
            before = links[0]

            with dve.Fori(0, B) as it:
                links[0] = 0
                link = chained(it * LINKS_B + before)
                prev = (it + (B - 1)) % B

                def lo_of(key, k, c, signal):
                    dve.wait_ge(hi_done, C + it * 2 * C + k + 1)
                    dve.tensor_tensor(xT[1][:, c, :], psum[banks.place[key][0]][:, :], xT[0][:, c, :], ALU.subtract)\
                        .then_inc(signal, 1)

                for n in range(STEPS):
                    if n == NF:
                        for t in range(T):
                            dve.wait_ge(acc_full, it * 2 * T + t + 1)
                            dve.wait_ge(x2b_ready, it * T + t + 1)
                            dve.scalar_tensor_tensor(out=x2[:, t, :], in0=psum[t][:, :], scalar=1.0 / WS,
                                                     in1=x2[:, t, :], op0=ALU.mult, op1=ALU.add).then_inc(x3_ready, 1)
                        for c in range(C):
                            lo_of(("x3T", c), c, c, x3T_split)
                        total(it, dt[:, bass.ds(prev, 1)], 2, None)
                    dve.wait_ge(gelu_ready, 1 + it * STEPS + n + 1)
                    if n >= 4 and (n - 4) % NF != NF - 1:
                        dve.wait_ge(down_done, it * (STEPS - 2) + downs(n - 4))
                    link(dve.tensor_copy(gT[0][:, n % 4, :], g32[:, n % 2, :]))
                    dve.tensor_tensor(gT[1][:, n % 4, :], g32[:, n % 2, :], gT[0][:, n % 4, :], ALU.subtract)\
                        .then_inc(g_split, 1)
                    for k in range(NF):
                        if CHUNK[k] == n:
                            dve.wait_ge(chunk_hi, it * NF + k + 1)
                            dve.scalar_tensor_tensor(out=wl[1][:, k % NW, :], in0=raw[:, k % 2, :], scalar=WS,
                                                     in1=wl[0][:, k % NW, :], op0=ALU.mult, op1=ALU.subtract)\
                                .then_inc(chunk_split, 1)
                    if n < 3:
                        norm3(link, it, n)
                    if n in ALPHA:
                        alpha(link, it, ALPHA.index(n))
                    if n in BETA:
                        beta(link, it, BETA.index(n))
                    if n in SUM and n != NF:
                        total(it, dt[:, bass.ds(prev, 1)], SUM.index(n), None)
                    if n == NORM2:
                        dve.wait_ge(x2_in, it * 16 + 32)
                        for t in range(T):
                            norm_stats(link, x2n, t)
                    if n == NORM2 + 1:
                        norm_rstd(link, 1e-5)
                    if n in (NORM2 + 2, NORM2 + 3):
                        for t in range(2 * (n - NORM2 - 2), 2 * (n - NORM2 - 1)):
                            norm_scale(link, h2, x2n, g2[:, :], t, scaled2)
                for c in range(C):
                    lo_of(("h2T", c), C + c, c, h2T_split)
                for t in range(T):
                    dve.wait_ge(acc_full, it * 2 * T + T + t + 1)
                    dve.wait_ge(x3b_ready, it * T + t + 1)
                    dve.scalar_tensor_tensor(out=f[:, t, :], in0=psum[t][:, :], scalar=1.0 / WS, in1=x2[:, t, :],
                                             op0=ALU.mult, op1=ALU.add).then_inc(r_ready, 1)
                dve.wait_ge(r_ready, 1 + it * T + T)
            assert links[0] == LINKS_B, [1, links[0]]
            link = chained(B * LINKS_B + before)
            links[0] = 0
            for part in range(3):
                norm3(link, B, part)
            for t in range(T):
                alpha(link, B, t)
            for t in range(T):
                beta(link, B, t)
                total(B, dt[:, B - 1:B], t, psum[t])


def four_layers(nc, a, out):
    ada_rows = nc.dram_tensor("ada_rows", (B, 2 * D), F32).ap()
    x2 = nc.dram_tensor("x2_rows", (B, S, D), F32).ap()
    ada_embedding(nc, a, ada_rows)
    attention_pass(nc, a, ada_rows, x2)
    ffn_pass(nc, a, x2, out)


def stencil_blocks():
    d1, d2 = np.zeros((S, S)), np.zeros((S, S))
    for i in range(1, S - 1):
        d1[i, i - 1:i + 2] = -0.5, 0, 0.5
        d2[i, i - 1:i + 2] = 0.5, -1, 0.5
    d1[0, :3] = -1.5, 2, -0.5
    d1[-1, -3:] = 0.5, -2, 1.5
    d2[0, :4] = 1, -2.5, 2, -0.5
    d2[-1, -4:] = -0.5, 2, -2.5, 1
    cut = [m[i * P:(i + 1) * P, j * P:(j + 1) * P].T
           for m in (d1, d2) for i, j in ((0, 0), (1, 1), (T - 1, T - 1), (1, 0), (1, 2))]
    return np.stack(cut, 1).astype(np.float16)


def laid_out(inputs):
    w = {n: np.ascontiguousarray(np.asarray(v)) for n, v in inputs.items()}
    col = lambda v: v.reshape(-1, P).T
    half = D // 2
    a = {
        "x": w["x"], "dom": w["itok_B_0_15"], "steps": w["itok_B_34_63"], "idx2": w["itok_B_0_7"],
        "dt": w["condB_dt"], "bias": w["fside_Bx16xSxS_0"], "mask": w["mask_Bx1xSxS_bk0"][:, 0],
        "freqs": col(np.exp(np.arange(half, dtype=np.float32) * np.float32(-math.log(10000.0) / (half - 1)))),
        "dmat": stencil_blocks(),
        "exp_WT": w["L0_cond_expert_W"].transpose(0, 2, 1),
        "exp_vec": np.stack([w["L0_cond_expert_b"], w["L0_cond_domain_emb"]], -1),
        "down_WT": w["L0_cond_down_W"].T.reshape(C, P, A).transpose(1, 0, 2),
        "up_WT": w["L0_cond_up_W"].T,
        "down_b": col(w["L0_cond_down_b"]), "up_b": w["L0_cond_up_b"],
        "ln_g": w["L0_cond_ln_gamma"], "ln_b": w["L0_cond_ln_beta"],
        "W_l2": np.concatenate([
            w["L2_cond_Wi"].reshape(NE2, C, P, NF, P).transpose(0, 3, 2, 1, 4).reshape(NE2, NF, P, D),
            w["L2_cond_Wo"].reshape(NE2, NF, P, D)], -1),
        "bi": w["L2_cond_bi"].reshape(NE2, NF, P).transpose(0, 2, 1),
        "rows2": np.stack([w["L2_cond_bo"], w["L2_cond_gamma"], w["L2_cond_beta"]], 1),
        "grids": np.concatenate([w["L3_cond_A_grid"], w["L3_cond_B_grid"]], 0),
    }
    for n in ("W_ada", "b_ada", "Wq", "Wk", "Wv", "Wo", "bo", "W1", "W2", "b2", "g2", "beta2"):
        a[n] = w["L1_cond_" + n]
    for n in ("bq", "bk", "bv", "b1"):
        a[n] = col(w["L1_cond_" + n])
    return {n: np.ascontiguousarray(v) for n, v in a.items()}


def kernel(**inputs):
    import concourse.bacc as bacc
    from concourse.bass_utils import run_bass_kernel_spmd

    nc = bacc.Bacc("TRN2", target_bir_lowering=False, num_devices=1)
    arrays = {"in_" + n: v for n, v in laid_out(inputs).items()}
    a = {n[3:]: nc.dram_tensor(n, v.shape, mybir.dt.from_np(v.dtype), kind="ExternalInput").ap()
         for n, v in arrays.items()}
    out = nc.dram_tensor("out", (B, S, D), F32, kind="ExternalOutput").ap()
    four_layers(nc, a, out)
    return run_bass_kernel_spmd(nc, [arrays], core_ids=[0]).results[0]["out"]
```

```python
import math
from contextlib import ExitStack

import numpy as np

import concourse.bass as bass
from concourse import mybir

ALU = mybir.AluOpType
ACT = mybir.ActivationFunctionType
F32 = mybir.dt.float32
F16 = mybir.dt.float16
BF16 = mybir.dt.bfloat16
I32 = mybir.dt.int32
U8 = mybir.dt.uint8

LINKS_A = 30
LINKS_B = 134
P = 128
B, S, D = 8, 512, 512
T = S // P
C = D // P
NE0, A = 16, 128
H, HD = 16, 32
G = H // 4
FF = 2048
NF = FF // P
NE2 = 8
WS = 256.0
NEG = -1.0e30
PS = 4096.0
RSQRT_SEED = 1597463007.0
MAGIC = 12582912.0
TWO_PI = (6.28125, 0.0019350051879882812, 3.0199159819567e-07)


class Banks:

    def __init__(self, order, unsignalled=()):
        self.uses = [0] * 8
        self.place = {}
        last = {bank: key for key, bank in order}
        self.first, seen = {}, set()
        for key, bank in order:
            self.first[key] = bank not in seen
            seen.add(bank)
            self.place[key] = (bank, self.uses[bank], last[bank])
            self.uses[bank] += key[0] not in unsignalled
            last[bank] = key


def rsqrt_steps(dve, link, v, y, a, seed_bits, v_bits, fused=True):
    link(dve.tensor_scalar(seed_bits, v_bits, -0.5, RSQRT_SEED, ALU.mult, ALU.add))
    for _ in range(3):
        link(dve.tensor_tensor(a, y, y, ALU.mult))
        if not fused:
            link(dve.tensor_tensor(a, a, v, ALU.mult))
            link(dve.tensor_scalar(a, a, -0.5, 1.5, ALU.mult, ALU.add))
            link(dve.tensor_tensor(y, a, y, ALU.mult))
            continue
        link(dve.scalar_tensor_tensor(out=a, in0=a, scalar=-0.5, in1=v, op0=ALU.mult, op1=ALU.mult))
        link(dve.scalar_tensor_tensor(out=y, in0=a, scalar=1.5, in1=y, op0=ALU.add, op1=ALU.mult))


HT = H * T
LAG_T = 5
LAG_PV = 7
SLOTS_ALL = HT + 11


def rinv_slot(g):
    return 4 * T * (g + 1) + 2


def turn_slot(g):
    return 4 * T * (g + 1) + 4


def ctx_slot(g):
    return 4 * T * (g + 1) + LAG_PV + 2


PE_L0 = {4: ("expert",)} | {8 + 2 * t: ("up", t) for t in range(T)}
ACT_L0 = {5: ("expert",)} | {31 + 2 * t: ("scale0", t) for t in range(T)} \
    | {56 + 2 * t: ("scale1", t) for t in range(T)}
DVE_L0 = {2: ("g",), 6: ("e",)} | {9 + 2 * t: ("y", t) for t in range(T)} \
    | {19 + 2 * t: ("stats0", t) for t in range(T)} | {45 + 2 * t: ("stats1", t) for t in range(T)}


def attention_slots():
    order, ring = [], 0
    for n in range(SLOTS_ALL):
        if n < HT:
            order.append((("S", n // T, n % T), n % 3))
        if n in PE_L0:
            order.append((PE_L0[n], 3 + ring % 3))
            ring += 1
        if 0 <= n - LAG_T < HT:
            m = n - LAG_T
            order.append((("T", m // T, m % T), 3 + ring % 3))
            ring += 1
        if 0 <= n - LAG_PV < HT and (n - LAG_PV) % (4 * T) == 0:
            g = (n - LAG_PV) // (4 * T)
            order.append((("ctx", g), 6 + g % 2))
        for g in range(G):
            if n == turn_slot(g):
                order.append((("R", g), 3 + ring % 3))
                ring += 1
    return order


def attention_pass(nc, a, ada_rows, x2_dram):
    order = [(("q", c), c) for c in range(C)]
    order += [(("k", c), 4 + c) for c in range(C)]
    order += [(("v", t), t) for t in range(2)]
    order += [(("xT", c), 4 + c) for c in range(C)]
    order += [(("v", t), t) for t in range(2, T)] + [(("down",), 4)]
    order += attention_slots()
    order += [(("x1T", c), 3 + c) for c in range(C)]
    order += [(("wo", t), (0, 1, 2, 7)[t]) for t in range(T)]
    banks = Banks(order, ("ctx",))

    with ExitStack() as ctx:
        def sb(name, shape, dt):
            return ctx.enter_context(nc.sbuf_tensor(name, shape, dt))

        def sem(name):
            return ctx.enter_context(nc.semaphore(name))

        wq, wk, wv, wo = ([sb(f"w{n}_{h}", [P, C, D], F16) for h in ("hi", "lo")] for n in "qkvo")
        wdown = [sb(f"wdown_{h}", [P, C, A], F16) for h in ("hi", "lo")]
        wup = [sb(f"wup_{h}", [P, D], F16) for h in ("hi", "lo")]
        wexp = [sb(f"wexp_{h}", [P, A], F16) for h in ("hi", "lo")]
        ident = sb("ident", [P, P], F32)
        ident_bf = sb("ident_bf", [P, P], BF16)
        down_b = sb("down_b", [P, 1], F32)
        bq, bk, bv = (sb(f"b{n}", [P, C], F32) for n in "qkv")
        up_b, ln_g, ln_b, bo = (sb(n, [P, D], F32) for n in ("up_b", "ln_g", "ln_b", "bo"))
        ada = sb("ada", [P, 2, D], F32)
        dom = sb("dom", [P, B], I32)
        dom_f = sb("dom_f", [P, B], F32)
        valid = sb("valid", [P, B], F32)
        invalid = sb("invalid", [P, B], F32)
        dom_at = sb("dom_at", [1, B], I32)
        exp_raw = sb("exp_raw", [P, A], F32)
        exp_eff = sb("exp_eff", [P, A], F32)
        exp_vec = sb("exp_vec", [P, 2], F32)
        exp_bias = sb("exp_bias", [P, 1], F32)
        xin = sb("xin", [P, T, D], F32)
        x1 = sb("x1", [P, T, D], F32)
        xT = [sb(f"xT_{h}", [P, C, S], F16) for h in ("hi", "lo")]
        q_st = sb("q_st", [P, H, S], F16)
        k_st = sb("k_st", [P, H, S], F16)
        v_pad = [sb(f"v_{h}", [P, T, H, P], F16) for h in ("hi", "lo")]
        mask_raw = sb("mask_raw", [P, T, S], U8)
        mask_add = sb("mask_add", [P, T, S], BF16)
        NB = 4
        bias = sb("bias", [P, NB, 2, S], F32)
        NT = 4
        negs = sb("negs", [P, NT, S], F32)
        nmax = sb("nmax", [P, 2, T], F32)
        rsum = sb("rsum", [P, T, H], F32)
        rinv = sb("rinv", [P, T, 4], F32)
        rinv_x = sb("rinv_x", [P, T, P], F32)
        rinv_T = sb("rinv_T", [P, S], F32)
        ctx32 = sb("ctx32", [P, S], F32)
        prob = sb("prob", [P, 2, T, S], F32)
        pT = [sb(f"pT_{h}", [P, 2, T, S], F16) for h in ("hi", "lo")]
        qT = [pT[h][:, 0, :, :] for h in range(2)]
        kT = [pT[h][:, 1, :, :] for h in range(2)]
        hid32 = rinv_T
        hT = [ctx32[:, h * D // 2:(h + 1) * D // 2].bitcast(F16) for h in range(2)]
        f32t = negs
        raw = prob
        x1T = [prob[:, 0, 2 * h:2 * h + 2, :].rearrange("p t s -> p (t s)").bitcast(F16)
               .rearrange("p (c s) -> p c s", c=C) for h in range(2)]
        steps_i = sb("steps_i", [P, B], I32)
        steps = sb("steps", [P, B], F32)
        freq = sb("freq", [P, 2], F32)
        ang = sb("ang", [P, C, B], F32)
        turns = sb("turns", [P, C, B], F32)
        emb = sb("emb", [P, C, B], F32)
        w_ada = bias[:, :, :, :].rearrange("p n t s -> p n (t s)")
        b_ada = x1[0:B, 0:2, :].rearrange("p t d -> p (t d)")
        rows = x1[0:B, 2:4, :].rearrange("p t d -> p (t d)")
        stats = sb("stats", [P, T, 6], F32)
        mv = sb("mv", [P, T, 2], F32)
        var = sb("var", [P, T], F32)
        rstd = sb("rstd", [P, T], F32)
        shift = sb("shift", [P, T], F32)
        newt = sb("newt", [P, T], F32)

        psum = [ctx.enter_context(nc.psum_tensor(f"bank{i}", [P, S], F32)) for i in range(8)]
        full = [sem(f"bank{i}_full") for i in range(8)]

        raw_in = [sem(f"raw{i}_in") for i in range(2)]
        vec_in = sem("vec_in")
        dom_in = sem("dom_in")
        dom_clipped = sem("dom_clipped")
        ident_set = sem("ident_set")
        weights_split = sem("weights_split")
        v_zeroed = sem("v_zeroed")
        x_in = sem("x_in")
        mask_in = sem("mask_in")
        expert_in = sem("expert_in")
        ada_in = sem("ada_in")
        bias_in = [sem(f"bias{i}_in") for i in range(NB)]
        mask_ready = sem("mask_ready")
        expert_ready = sem("expert_ready")
        hi_done = sem("hi_done")
        x_hi = sem("x_hi")
        x1_hi = sem("x1_hi")
        stats_ready = sem("stats_ready")
        first_full = sem("first_tiles_full")
        weights_hi = sem("weights_hi")
        hid_ready = sem("hid_ready")
        steps_in = sem("steps_in")
        w_ada_in = sem("w_ada_in")
        angles_reduced = sem("angles_reduced")
        emb_ready = sem("emb_ready")
        ada_full = sem("ada_full")
        rows_ready = sem("ada_rows_ready")
        rows_out = sem("ada_rows_out")
        pool_chain = sem("pool_chain")
        pool_carrier = sem("pool_wait_carrier")
        xT_split = sem("xT_split")
        x1T_split = sem("x1T_split")
        f32_ready = sem("f32_ready")
        g_split = sem("g_split")
        e_split = sem("e_split")
        qk_split = sem("qk_split")
        v_split = sem("v_split")
        qk_stacked = sem("qk_stacked")
        xb_ready = sem("xb_ready")
        y_ready = sem("y_ready")
        scored = sem("scored")
        rstd_ready = sem("rstd_ready")
        gained = sem("gained")
        scaled0 = sem("scaled0")
        ln0_ready = sem("ln0_ready")
        scaled1 = sem("scaled1")
        x1_ready = sem("x1_ready")
        x1b_ready = sem("x1b_ready")
        prob_ready = sem("prob_ready")
        pT_split = sem("pT_split")
        pv_done = sem("pv_done")
        rinv_ready = sem("rinv_ready")
        rinv_T_ready = sem("rinv_T_ready")
        ctx_ready = sem("ctx_ready")
        ctx_hi = sem("ctx_hi")
        ctx_split = sem("ctx_split")
        x2_ready = sem("x2_ready")
        x2_out = sem("x2_out")
        chain = sem("dve_chain")
        carrier = sem("wait_carrier")

        block = ctx.enter_context(nc.Block())

        BEGUN = {"vector": (x2_ready, pT_split, ctx_ready, scored, v_split, ctx_split),
                 "scalar": (x2_out, prob_ready), "tensor": (pv_done,)}
        base = {s: 1 for sems in BEGUN.values() for s in sems}
        base |= {xT_split: C, hid_ready: 2, y_ready: T, x1T_split: C}

        def begin(eng, name):
            for s in BEGUN[name]:
                eng.sem_inc(s, 1)

        def read_by(key):
            name, k = key[0], key[-1]
            return {"xT": (xT_split, C, k), "down": (hid_ready, 2, 0), "expert": (hid_ready, 2, 1),
                    "up": (y_ready, T, k), "x1T": (x1T_split, C, k), "q": (f32_ready, 12, 0),
                    "k": (f32_ready, 12, 4), "v": (f32_ready, 12, 8), "S": (scored, H * T, k),
                    "T": (pT_split, H * T, k), "R": (rinv_T_ready, G, k), "ctx": (ctx_ready, G, k),
                    "wo": (x2_ready, T, k)}[name]

        def claim(pe, it, key):
            bank, _, last = banks.place[key]
            signal, per, k = read_by(last)
            if last[0] in ("q", "k", "v"):
                k += last[1]
            if last[0] in ("S", "T"):
                k += last[1] * T
            pe.wait_ge(signal, base.get(signal, 0) + it * per + (0 if banks.first[key] else k + 1))
            return psum[bank]

        def arrived(eng, it, key):
            bank, before, _ = banks.place[key]
            eng.wait_ge(full[bank], it * banks.uses[bank] + before + 1)
            return psum[bank]

        def full_of(key):
            return full[banks.place[key][0]]

        def f32_split(n):
            return (qk_split, 2 * C, n + 1) if n < 8 else (v_split, T, n - 7)

        FIRST = [("xT", c) for c in range(C)] + [("down",), ("expert",)] + [("up", t) for t in range(T)]
        FIRST += [("x1T", c) for c in range(C)]
        FIRST_BANK = {key: i if i < 6 else i - 6 for i, key in enumerate(FIRST)}

        def before_it(it):
            return 0 if it is None else it + 1

        def l0_tile(eng, it, key):
            if it is None:
                eng.wait_ge(first_full, FIRST.index(key) + 1)
                return psum[FIRST_BANK[key]]
            return arrived(eng, it, key)

        WEIGHTS = [("down_WT", wdown), ("up_WT", wup), ("Wq", wq), ("Wk", wk), ("Wv", wv), ("Wo", wo)]
        VECS = [(down_b[:, :], a["down_b"]), (bq[:, :], a["bq"]), (bk[:, :], a["bk"]), (bv[:, :], a["bv"]),
                (up_b[:, :], a["up_b"].partition_broadcast(P)), (ln_g[:, :], a["ln_g"].partition_broadcast(P)),
                (ln_b[:, :], a["ln_b"].partition_broadcast(P)), (bo[:, :], a["bo"].partition_broadcast(P))]
        SLOTS = [(0, 0, 0), (1, 1, 0), (2, 0, 1)]

        def weight_view(tile):
            return tile[:, :, :] if len(tile.shape) == 3 else tile[:, :]

        def raw_view(i, tile):
            n = tile.shape[-1] * (tile.shape[1] if len(tile.shape) == 3 else 1)
            v = raw[:, i % 2, :, :].rearrange("p t s -> p (t s)")[:, 0:n]
            return v.rearrange("p (c n) -> p c n", c=tile.shape[1]) if len(tile.shape) == 3 else v

        @block.sync
        def _(sp):
            sp.dma_start(steps_i[:, :], a["steps"].partition_broadcast(P)).then_inc(steps_in, 16)
            sp.dma_start(freq[:, :], a["freqs"]).then_inc(steps_in, 16)
            sp.dma_start(dom[:, :], a["dom"].partition_broadcast(P)).then_inc(dom_in, 16)

            def load_x(seq):
                sp.dma_start(xin[:, :, :], a["x"][seq].rearrange("(t p) d -> p t d", p=P)).then_inc(x_in, 16)

            def load_expert(at):
                e = sp.value_load(dom_at[0:1, at], min_val=0, max_val=NE0 - 1)
                sp.dma_start(exp_raw[:, :], a["exp_WT"][e]).then_inc(expert_in, 16)
                sp.dma_start(exp_vec[:, :], a["exp_vec"][e]).then_inc(expert_in, 16)

            def load_ada(seq):
                sp.dma_start(ada[:, :, :], ada_rows[seq].rearrange("(k d) -> k d", k=2).partition_broadcast(P)).then_inc(ada_in, 16)

            def load_mask(seq):
                sp.dma_start(mask_raw[:, :, :], a["mask"][seq].rearrange("(t p) s -> p t s", p=P)).then_inc(mask_in, 16)

            def load_weight(i):
                name, (hi, _) = WEIGHTS[i]
                if i >= 2:
                    sp.wait_ge(weights_split, i - 1)
                src = a[name]
                if len(hi.shape) == 3 and name != "down_WT":
                    src = src.rearrange("(c p) n -> p c n", p=P)
                sp.dma_start(raw_view(i, hi), src).then_inc(raw_in[i % 2], 16)

            load_x(0)
            load_weight(0)
            load_weight(1)
            sp.wait_ge(dom_clipped, 1)
            load_expert(slice(0, 1))
            for dst, src in VECS:
                sp.dma_start(dst, src).then_inc(vec_in, 16)
            sp.dma_start(w_ada, a["W_ada"].rearrange("(c p) n -> p c n", p=P)).then_inc(w_ada_in, 16)
            sp.dma_start(b_ada, a["b_ada"].partition_broadcast(B)).then_inc(w_ada_in, 16)
            load_mask(0)
            load_weight(2)
            load_weight(3)
            sp.wait_ge(rows_ready, 3)
            sp.dma_start(ada_rows, rows).then_inc(rows_out, 16)
            sp.wait_ge(rows_out, 16)
            load_ada(0)
            load_weight(4)
            load_weight(5)
            with sp.Fori(0, B) as it:
                nxt = (it + 1) % B

                def load_bias(n):
                    sp.wait_ge(scored, 1 + it * (T * H) + max(0, 2 * (n - NB) + 2))
                    h, j = n // 2, n % 2
                    src = a["bias"][it, h, j * 2 * P:(j + 1) * 2 * P, :].rearrange("(t p) s -> p t s", p=P)
                    sp.dma_start(bias[:, n % NB, :, :], src).then_inc(bias_in[n % NB], 16)

                for n in range(NB):
                    load_bias(n)
                sp.wait_ge(x1b_ready, it * T + T)
                sp.wait_ge(x1_hi, it * C + C)
                load_x(nxt)
                sp.wait_ge(x1_ready, it * T + T)
                load_expert(bass.ds(nxt, 1))
                load_ada(nxt)
                sp.wait_ge(mask_ready, it * 1 + 1)
                load_mask(nxt)
                for which, (parts, stack) in enumerate(((qT, q_st), (kT, k_st))):
                    sp.wait_ge(qk_split, it * 2 * C + (which + 1) * C)
                    for i in range(4):
                        for slot in SLOTS:
                            sp.dma_start(
                                stack[32 * slot[0]:32 * slot[0] + 32, :, :].rearrange("p (c i) s -> p i c s", i=4)[:, i],
                                parts[slot[1 + which]][32 * i:32 * i + 32, :, :]).then_inc(qk_stacked, 16)
                for n in range(NB, 2 * H):
                    load_bias(n)

        @block.gpsimd
        def _(pool):
            pool.memset(ident[:, :], 0.0).then_inc(ident_set, 1)
            pool.wait_ge(ident_set, 1)
            pool.affine_select(out=ident[:, :], in_=ident[:, :], compare_op=ALU.not_equal, fill=1.0, base=0,
                               pattern=[[-1, P]], channel_multiplier=1).then_inc(ident_set, 1)
            pool.wait_ge(ident_set, 2)
            pool.tensor_copy(ident_bf[:, :], ident[:, :]).then_inc(ident_set, 1)
            for part in v_pad:
                pool.memset(part[:, :, :, :].rearrange("p t h m -> p (t h m)").bitcast(F32), 0.0).then_inc(v_zeroed, 1)
            pool.wait_ge(vec_in, 16 * len(VECS))
            count = [0]

            def pool_link(base, ins):
                count[0] += 1
                ins.then_inc(pool_chain, 1)
                pool.wait_ge(pool_chain, base + count[0])

            def rstd_of_norm(base, q, which):
                def link(ins):
                    pool_link(base, ins)
                    pool.sem_inc(pool_carrier, 1)
                pool.wait_ge(stats_ready, q * (2 * T) + (which + 1) * T)
                pool.sem_inc(pool_carrier, 1)
                link(pool.tensor_scalar(var[:, :], mv[:, :, 1], 1e-5, None, ALU.add))
                rsqrt_steps(pool, link, var[:, :], rstd[:, :], newt[:, :], rstd[:, :].bitcast(I32),
                            var[:, :].bitcast(I32), fused=False)
                link(pool.tensor_scalar(newt[:, :], mv[:, :, 0], -1.0, None, ALU.mult))
                pool.tensor_tensor(shift[:, :], newt[:, :], rstd[:, :], ALU.mult).then_inc(rstd_ready, 1)

            def finish_x1(it):
                q = before_it(it)
                base = 0 if it is None else before_loop + it * POOL_LINKS
                count[0] = 0
                pool.wait_ge(x_in, q * 16 + 16)
                l0_tile(pool, it, ("xT", C - 1))
                for t in range(T):
                    pool.tensor_tensor(xin[:, t, :], xin[:, t, :], up_b[:, :], ALU.add).then_inc(xb_ready, 1)
                rstd_of_norm(base, q, 0)
                for t in range(T):
                    if it is None:
                        pool.wait_ge(gained, t + 1)
                    else:
                        pool.wait_ge(scaled0, q * T + t + 1)
                        pool_link(base, pool.tensor_tensor(xin[:, t, :], xin[:, t, :], ln_g[:, :], ALU.mult))
                    pool.tensor_tensor(xin[:, t, :], xin[:, t, :], ln_b[:, :], ALU.add).then_inc(ln0_ready, 1)
                rstd_of_norm(base, q, 1)
                pool.wait_ge(ada_in, q * 16 + 16)
                for t in range(T):
                    if it is None:
                        pool.wait_ge(gained, T + t + 1)
                    else:
                        pool.wait_ge(scaled1, q * T + t + 1)
                        pool_link(base, pool.tensor_tensor(xin[:, t, :], xin[:, t, :], ada[:, 0, :], ALU.mult))
                    pool.tensor_tensor(xin[:, t, :], xin[:, t, :], ada[:, 1, :], ALU.add).then_inc(x1_ready, 1)

            finish_x1(None)
            before_loop = count[0]
            POOL_LINKS = before_loop + 2 * T
            pool.wait_ge(rows_out, 16)
            with pool.Fori(0, B) as it:
                pool.wait_ge(x2_out, 1 + it * 64)
                for t in range(T):
                    pool.wait_ge(x1_ready, it * T + t + 1)
                    pool.tensor_tensor(x1[:, t, :], xin[:, t, :], bo[:, :], ALU.add).then_inc(x1b_ready, 1)
                finish_x1(it)

        @block.tensor
        def _(pe):
            begin(pe, "tensor")
            pe.wait_ge(ident_set, 3)

            def three(out, w, x, first, last):
                pe.matmul(out, w[0], x[0], start=first, stop=False)
                pe.matmul(out, w[0], x[1], start=False, stop=False)
                return pe.matmul(out, w[1], x[0], start=False, stop=last)

            def transposes(bank, c):
                for t in range(T):
                    mm = pe.transpose(bank[:, t * P:(t + 1) * P], xin[:, t, c * P:(c + 1) * P], ident[:, :])
                return mm

            def l0_products(it, key):
                q = before_it(it)
                name, i = key[0], key[-1]
                bank = psum[FIRST_BANK[key]] if it is None else claim(pe, it, key)
                if name == "xT":
                    pe.wait_ge(x_in, q * 16 + 16)
                    mm = transposes(bank, i)
                if name == "x1T":
                    pe.wait_ge(x1_ready, q * T + T)
                    mm = transposes(bank, i)
                if name == "down":
                    pe.wait_ge(xT_split, q * C + C)
                    for c in range(C):
                        mm = three(bank[:, :], [w[:, c, :] for w in wdown], [x[:, c, :] for x in xT], c == 0, c == C - 1)
                if name == "expert":
                    pe.wait_ge(expert_ready, q + 1)
                    pe.wait_ge(g_split, q + 1)
                    mm = three(bank[:, :], [w[:, :] for w in wexp], hT, True, True)
                if name == "up":
                    pe.wait_ge(e_split, q + 1)
                    mm = three(bank[:, :], [x[:, i * P:(i + 1) * P] for x in hT], [w[:, :] for w in wup], True, True)
                mm.then_inc(first_full if it is None else full_of(key), 1)

            for key in FIRST[:-C]:
                if key == ("down",):
                    pe.wait_ge(weights_split, 2)
                l0_products(None, key)
            pe.wait_ge(emb_ready, 2)
            pe.wait_ge(w_ada_in, 32)
            for i in range(2):
                for c in range(C):
                    mm = pe.matmul(psum[6 + i][0:B, :], emb[:, c, :], w_ada[:, c, i * D:(i + 1) * D],
                                   start=(c == 0), stop=(c == C - 1))
                mm.then_inc(ada_full, 1)
            for key in FIRST[-C:]:
                l0_products(None, key)
            pe.wait_ge(weights_split, len(WEIGHTS))
            pe.wait_ge(v_zeroed, 2)
            with pe.Fori(0, B) as it:
                pe.wait_ge(x1T_split, it * C + C)
                for name, w in (("q", wq), ("k", wk)):
                    for m in range(C):
                        bank = claim(pe, it, (name, m))
                        for c in range(C):
                            mm = three(bank[:, :], [p[:, c, m * P:(m + 1) * P] for p in w],
                                       [x[:, c, :] for x in x1T], c == 0, c == C - 1)
                        mm.then_inc(full_of((name, m)), 1)
                for t in range(T):
                    if t == 2:
                        for c in range(C):
                            l0_products(it, ("xT", c))
                    bank = claim(pe, it, ("v", t))
                    for c in range(C):
                        mm = three(bank[:, :], [x[:, c, t * P:(t + 1) * P] for x in x1T],
                                   [p[:, c, :] for p in wv], c == 0, c == C - 1)
                    mm.then_inc(full_of(("v", t)), 1)

                l0_products(it, ("down",))

                pe.wait_ge(mask_ready, it * 1 + 1)
                pe.wait_ge(qk_stacked, it * 384 + 384)
                for n in range(SLOTS_ALL):
                    if n < HT:
                        h, j = n // T, n % T
                        bank = claim(pe, it, ("S", h, j))
                        pe.matmul(bank[:, :], ident_bf[:, :], mask_add[:, j, :], start=True, stop=False)
                        pe.matmul(bank[:, :], q_st[0:96, h, j * P:(j + 1) * P], k_st[0:96, h, :],
                                  start=False, stop=True).then_inc(full_of(("S", h, j)), 1)
                    if n in PE_L0:
                        l0_products(it, PE_L0[n])
                    if 0 <= n - LAG_T < HT:
                        h, j = (n - LAG_T) // T, (n - LAG_T) % T
                        if j == 0:
                            pe.wait_ge(prob_ready, 1 + it * HT + T * (h + 1))
                        bank = claim(pe, it, ("T", h, j))
                        for t in range(T):
                            mm = pe.transpose(bank[:, t * P:(t + 1) * P], prob[:, h % 2, t, j * P:(j + 1) * P],
                                              ident[:, :])
                        mm.then_inc(full_of(("T", h, j)), 1)
                    if 0 <= n - LAG_PV < HT:
                        h, j = (n - LAG_PV) // T, (n - LAG_PV) % T
                        key = ("ctx", h // 4)
                        if h % 4 == 0 and j == 0:
                            claim(pe, it, key)
                            pe.wait_ge(v_split, 1 + it * T + T)
                        bank = psum[banks.place[key][0]]
                        pe.wait_ge(pT_split, 1 + it * HT + T * h + j + 1)
                        mm = three(bank[:, :], [v[:, j, h, :] for v in v_pad], [p[:, h % 2, j, :] for p in pT],
                                   h % 4 == 0 and j == 0, h % 4 == 3 and j == T - 1)
                        if j == T - 1:
                            mm.then_inc(pv_done, 1)
                    for g in range(G):
                        if n == turn_slot(g):
                            bank = claim(pe, it, ("R", g))
                            pe.wait_ge(rinv_ready, it * G + g + 1)
                            for t in range(T):
                                mm = pe.transpose(bank[:, t * P:(t + 1) * P], rinv_x[:, t, :], ident[:, :])
                            mm.then_inc(full_of(("R", g)), 1)
                for c in range(C):
                    l0_products(it, ("x1T", c))
                into = [claim(pe, it, ("wo", t)) for t in range(T)]
                for c in range(C):
                    pe.wait_ge(ctx_split, 1 + it * G + c + 1)
                    for t in range(T):
                        mm = three(into[t][:, :], [x[:, c, t * P:(t + 1) * P] for x in xT],
                                   [p[:, c, :] for p in wo], c == 0, c == C - 1)
                        if c == C - 1:
                            mm.then_inc(full_of(("wo", t)), 1)

        @block.scalar
        def _(act):
            begin(act, "scalar")

            def l0_part(it, key):
                q = before_it(it)
                if key[0] == "xT":
                    bank = l0_tile(act, it, key)
                    act.activation(xT[0][:, key[1], :], bank[:, :], ACT.Copy).then_inc(x_hi, 1)
                if key[0] == "x1T":
                    bank = l0_tile(act, it, key)
                    act.activation(x1T[0][:, key[1], :], bank[:, :], ACT.Copy).then_inc(x1_hi, 1)
                if key[0] == "down":
                    bank = l0_tile(act, it, key)
                    act.activation(hid32[:, :], bank[:, :], ACT.Gelu, scale=1.0 / WS, bias=down_b[:, :])\
                        .then_inc(hid_ready, 1)
                if key[0] == "expert":
                    act.wait_ge(expert_ready, q + 1)
                    act.wait_ge(g_split, q + 1)
                    bank = l0_tile(act, it, key)
                    act.activation(hid32[:, :], bank[:, :], ACT.Identity, scale=1.0 / WS, bias=exp_bias[:, :])\
                        .then_inc(hid_ready, 1)

                if key[0] in ("scale0", "scale1"):
                    which, t = int(key[0] == "scale1"), key[1]
                    act.wait_ge(rstd_ready, q * 2 + which + 1)
                    act.activation(xin[:, t, :], xin[:, t, :], ACT.Identity, scale=rstd[:, t:t + 1],
                                   bias=shift[:, t:t + 1]).then_inc(scaled1 if which else scaled0, 1)

            def weight_hi(i):
                hi = WEIGHTS[i][1][0]
                act.wait_ge(raw_in[i % 2], 16 * (i // 2 + 1))
                act.activation(weight_view(hi), raw_view(i, hi), ACT.Copy, scale=WS).then_inc(weights_hi, 1)

            act.wait_ge(angles_reduced, 1)
            act.activation(ang[:, :, :], ang[:, :, :], ACT.Sin).then_inc(emb_ready, 1)
            act.wait_ge(emb_ready, 1)
            act.activation(emb[:, :, :], ang[:, :, :], ACT.Silu).then_inc(emb_ready, 1)
            weight_hi(0)
            weight_hi(1)
            act.wait_ge(vec_in, 16 * len(VECS))
            for key in FIRST[:C + 2]:
                l0_part(None, key)
            weight_hi(2)
            weight_hi(3)
            for t in range(T):
                l0_part(None, ("scale0", t))
            for t in range(T):
                l0_part(None, ("scale1", t))
            weight_hi(4)
            weight_hi(5)
            act.wait_ge(weights_split, len(WEIGHTS))
            for c in range(C):
                l0_part(None, ("x1T", c))
            with act.Fori(0, B) as it:
                def copy_hi(key, dst, scale):
                    bank = arrived(act, it, key)
                    act.activation(dst, bank[:, :], ACT.Copy, scale=scale).then_inc(hi_done, 1)

                def to_f32(n, key, func, scale, bias_ap):
                    bank = arrived(act, it, key)
                    split, per, k = f32_split(n - 2 if n >= 2 else 10 + n)
                    act.wait_ge(split, base.get(split, 0) + it * per + (k if n >= 2 else 0))
                    dst = f32t[:, n % 2, :]
                    if bias_ap is None:
                        ins = act.activation(dst, bank[:, :], func, scale=scale)
                    else:
                        ins = act.activation(dst, bank[:, :], func, scale=scale, bias=bias_ap)
                    ins.then_inc(f32_ready, 1)

                for m in range(C):
                    to_f32(m, ("q", m), ACT.Identity, 1.0 / (WS * math.sqrt(HD)), bq[:, m:m + 1])
                for m in range(C):
                    to_f32(C + m, ("k", m), ACT.Identity, 1.0 / WS, bk[:, m:m + 1])
                for t in range(T):
                    if t == 2:
                        for c in range(C):
                            l0_part(it, ("xT", c))
                    to_f32(2 * C + t, ("v", t), ACT.Copy, 1.0 / WS, None)
                l0_part(it, ("down",))
                for n in range(SLOTS_ALL):
                    if 0 <= n - LAG_T < HT:
                        h, j = (n - LAG_T) // T, (n - LAG_T) % T
                        if j == 0:
                            act.wait_ge(pv_done, 1 + it * H + max(0, h - 1))
                        copy_hi(("T", h, j), pT[0][:, h % 2, j, :], PS)
                    if n < HT:
                        h, j = n // T, n % T
                        act.wait_ge(scored, 1 + it * HT + n + 1)
                        act.activation(prob[:, h % 2, j, :], negs[:, j % NT, :], ACT.Exp, scale=-1.0,
                                       bias=nmax[:, h % 2, j:j + 1],
                                       accum_out=rsum[:, j, h:h + 1]).then_inc(prob_ready, 1)
                    if n in ACT_L0:
                        l0_part(it, ACT_L0[n])
                    for g in range(G):
                        if n == turn_slot(g) + 1:
                            bank = arrived(act, it, ("R", g))
                            act.wait_ge(ctx_ready, 1 + it * G + g)
                            act.wait_ge(e_split, it + 2)
                            act.activation(rinv_T[:, :], bank[:, :], ACT.Copy).then_inc(rinv_T_ready, 1)
                        if n == ctx_slot(g):
                            act.wait_ge(ctx_ready, 1 + it * G + g + 1)
                            act.activation(xT[0][:, g, :], ctx32[:, :], ACT.Identity, bias=bv[:, g:g + 1])\
                                .then_inc(ctx_hi, 1)
                for c in range(C):
                    l0_part(it, ("x1T", c))
                for t in range(T):
                    act.wait_ge(x2_ready, 1 + it * T + t + 1)
                    act.dma_start(x2_dram[it, t * P:(t + 1) * P, :], x1[:, t, :]).then_inc(x2_out, 16)
            act.wait_ge(x2_out, 1 + B * 64)

        @block.vector
        def _(dve):
            links = [0]

            def chained(base):
                def link(ins):
                    links[0] += 1
                    ins.then_inc(chain, 1)
                    dve.wait_ge(chain, base + links[0])
                return link

            begin(dve, "vector")
            link = chained(0)
            dve.wait_ge(steps_in, 32)
            link(dve.tensor_copy(steps[:, :], steps_i[:, :]))
            link(dve.tensor_scalar(steps[:, :], steps[:, :], 40.0, None, ALU.mult))
            for c in range(2):
                link(dve.tensor_scalar(ang[:, c, :], steps[:, :], freq[:, c:c + 1], None, ALU.mult))
            lo, k = ang[:, 0:2, :], turns[:, 0:2, :]
            link(dve.tensor_scalar(k, lo, 1.0 / (2.0 * math.pi), MAGIC, ALU.mult, ALU.add))
            link(dve.tensor_scalar(k, k, MAGIC, None, ALU.subtract))
            for part in TWO_PI:
                link(dve.scalar_tensor_tensor(out=lo, in0=k, scalar=-part, in1=lo, op0=ALU.mult, op1=ALU.add))
            hi, over = ang[:, 2:4, :], turns[:, 2:4, :]
            link(dve.tensor_scalar(hi, lo, math.pi / 2, None, ALU.add))
            link(dve.tensor_scalar(over, hi, math.pi, -2.0 * math.pi, ALU.is_gt, ALU.mult))
            link(dve.tensor_tensor(hi, hi, over, ALU.add))
            dve.tensor_scalar(ang[:, :, :], ang[:, :, :], -3.1415925, 3.1415925, ALU.max, ALU.min)\
                .then_inc(angles_reduced, 1)
            dve.wait_ge(dom_in, 16)
            link(dve.tensor_copy(dom_f[:, :], dom[:, :]))
            link(dve.tensor_scalar(valid[:, :], dom_f[:, :], 0.0, None, ALU.is_ge))
            link(dve.tensor_scalar(invalid[:, :], dom_f[:, :], float(NE0), None, ALU.is_lt))
            link(dve.tensor_tensor(valid[:, :], valid[:, :], invalid[:, :], ALU.mult))
            link(dve.tensor_scalar(invalid[:, :], valid[:, :], -1.0, 1.0, ALU.mult, ALU.add))
            dve.tensor_scalar(dom_at[:, :], dom[0:1, :], 0, NE0 - 1, ALU.max, ALU.min).then_inc(dom_clipped, 1)

            def weight_lo(i):
                hi, lo = WEIGHTS[i][1]
                dve.wait_ge(weights_hi, i + 1)
                dve.scalar_tensor_tensor(out=weight_view(lo), in0=raw_view(i, hi), scalar=WS, in1=weight_view(hi),
                                         op0=ALU.mult, op1=ALU.subtract).then_inc(weights_split, 1)

            def diagonal(v, t):
                part = v[:, t, :, :]
                return bass.AP(tensor=part.tensor, offset=part.offset,
                               ap=[list(part.ap[0]), [4 * P, G], [P + HD, 4], [1, HD]])

            def l0_part(link, it, part):
                q = before_it(it)
                name, i = part[0], part[-1]
                col = slice(0, 1) if it is None else bass.ds((it + 1) % B, 1)
                if name == "expert_weights":
                    dve.wait_ge(expert_in, q * 32 + 32)
                    link(dve.tensor_scalar(exp_eff[:, :], exp_raw[:, :], valid[:, col], None, ALU.mult))
                    link(dve.scalar_tensor_tensor(out=exp_eff[:, :], in0=ident[:, :], scalar=invalid[:, col],
                                                  in1=exp_eff[:, :], op0=ALU.mult, op1=ALU.add))
                    link(dve.tensor_scalar(wexp[0][:, :], exp_eff[:, :], WS, None, ALU.mult))
                    link(dve.scalar_tensor_tensor(out=wexp[1][:, :], in0=exp_eff[:, :], scalar=WS, in1=wexp[0][:, :],
                                                  op0=ALU.mult, op1=ALU.subtract))
                    dve.scalar_tensor_tensor(out=exp_bias[:, :], in0=exp_vec[:, 0:1], scalar=valid[:, col],
                                             in1=exp_vec[:, 1:2], op0=ALU.mult, op1=ALU.add).then_inc(expert_ready, 1)
                if name == "xT":
                    bank = psum[FIRST_BANK[part] if it is None else banks.place[part][0]]
                    dve.wait_ge(x_hi, q * C + i + 1)
                    dve.tensor_tensor(xT[1][:, i, :], bank[:, :], xT[0][:, i, :], ALU.subtract).then_inc(xT_split, 1)
                if name in ("g", "e"):
                    dve.wait_ge(hid_ready, q * 2 + (1 if name == "g" else 2))
                    link(dve.tensor_copy(hT[0], hid32[:, :]))
                    dve.tensor_tensor(hT[1], hid32[:, :], hT[0], ALU.subtract)\
                        .then_inc(g_split if name == "g" else e_split, 1)
                if name == "y":
                    bank = l0_tile(dve, it, ("up", i))
                    dve.wait_ge(xb_ready, q * T + i + 1)
                    dve.scalar_tensor_tensor(out=xin[:, i, :], in0=bank[:, :], scalar=1.0 / WS, in1=xin[:, i, :],
                                             op0=ALU.mult, op1=ALU.add).then_inc(y_ready, 1)
                if name in ("stats0", "stats1"):
                    dve.wait_ge(y_ready if name == "stats0" else ln0_ready, q * T + i + 1)
                    link(dve.bn_stats(stats[:, i, :], xin[:, i, :]))
                    dve.sem_inc(carrier, 1)
                    dve.bn_aggr(mv[:, i, :], stats[:, i, :]).then_inc(stats_ready, 1)
                if name == "x1T":
                    bank = psum[FIRST_BANK[part] if it is None else banks.place[part][0]]
                    dve.wait_ge(x1_hi, q * C + i + 1)
                    dve.tensor_tensor(x1T[1][:, i, :], bank[:, :], x1T[0][:, i, :], ALU.subtract).then_inc(x1T_split, 1)

            dve.wait_ge(ident_set, 2)
            dve.wait_ge(vec_in, 16 * len(VECS))
            for i in range(2):
                weight_lo(i)
            link(dve.tensor_scalar(bq[:, :], bq[:, :], 1.0 / math.sqrt(HD), None, ALU.mult))
            todo = list(range(2, len(WEIGHTS)))
            l0_part(link, None, ("expert_weights",))
            for c in range(C):
                l0_part(link, None, ("xT", c))
            for part in DVE_L0.values():
                l0_part(link, None, part)
                if part == ("stats0", T - 1):
                    for i in range(2):
                        dve.wait_ge(ada_full, i + 1)
                        dve.tensor_tensor(rows[:, i * D:(i + 1) * D], psum[6 + i][0:B, :], b_ada[:, i * D:(i + 1) * D],
                                          ALU.add).then_inc(rows_ready, 1)
                    dve.wait_ge(rows_ready, 2)
                    dve.tensor_scalar(rows[:, 0:D], rows[:, 0:D], 1.0, None, ALU.add).then_inc(rows_ready, 1)
                if part in (("stats0", T - 1), ("stats1", T - 1)):
                    which = int(part[0] == "stats1")
                    weight_lo(todo.pop(0))
                    if which:
                        dve.wait_ge(ada_in, 16)
                    for t in range(T):
                        dve.wait_ge((scaled0, scaled1)[which], t + 1)
                        dve.tensor_tensor(xin[:, t, :], xin[:, t, :], (ln_g[:, :], ada[:, 0, :])[which], ALU.mult)\
                            .then_inc(gained, 1)
            while todo:
                weight_lo(todo.pop(0))
            for c in range(C):
                l0_part(link, None, ("x1T", c))
            dve.wait_ge(v_zeroed, 2)
            before = links[0]

            with dve.Fori(0, B) as it:
                links[0] = 0
                link = chained(it * LINKS_A + before)

                def lo_of(key, k, hi, lo, signal, scale=None):
                    bank = psum[banks.place[key][0]]
                    dve.wait_ge(hi_done, it * (H * T) + k + 1)
                    if scale is None:
                        ins = dve.tensor_tensor(lo, bank[:, :], hi, ALU.subtract)
                    else:
                        ins = dve.scalar_tensor_tensor(out=lo, in0=bank[:, :], scalar=scale, in1=hi,
                                                       op0=ALU.mult, op1=ALU.subtract)
                    ins.then_inc(signal, 1)

                def split_f32(k, hi, lo, signal):
                    dve.wait_ge(f32_ready, it * 12 + k + 1)
                    src = f32t[:, k % 2, :]
                    link(dve.tensor_copy(hi, src))
                    dve.tensor_tensor(lo, src, hi, ALU.subtract).then_inc(signal, 1)

                dve.wait_ge(mask_in, it * 16 + 16)
                dve.tensor_scalar(mask_add[:, :, :], mask_raw[:, :, :], NEG, None, ALU.mult).then_inc(mask_ready, 1)
                for m in range(C):
                    split_f32(m, qT[0][:, m, :], qT[1][:, m, :], qk_split)
                l0_part(link, it, ("expert_weights",))
                for m in range(C):
                    split_f32(C + m, kT[0][:, m, :], kT[1][:, m, :], qk_split)
                for t in range(T):
                    if t == 2:
                        for c in range(C):
                            l0_part(link, it, ("xT", c))
                    dve.wait_ge(f32_ready, it * 12 + 2 * C + t + 1)
                    src = f32t[:, t % 2, :].rearrange("p (g i d) -> p g i d", i=4, d=HD)
                    hi, lo = (diagonal(v, t) for v in v_pad)
                    link(dve.tensor_copy(hi, src))
                    dve.tensor_tensor(lo, src, hi, ALU.subtract).then_inc(v_split, 1)
                dve.wait_ge(v_split, 1 + it * T + T)

                for n in range(SLOTS_ALL):
                    for g in range(G):
                        if n == rinv_slot(g):
                            dve.wait_ge(prob_ready, 1 + it * HT + 4 * T * (g + 1))
                            link(dve.reciprocal(rinv[:, :, :], rsum[:, :, 4 * g:4 * g + 4]))
                            dve.tensor_copy(rinv_x[:, :, :].rearrange("p t (i d) -> p t i d", d=HD),
                                            rinv[:, :, :].unsqueeze(3).to_broadcast([P, T, 4, HD]))\
                                .then_inc(rinv_ready, 1)
                        if n == ctx_slot(g):
                            bank = psum[banks.place["ctx", g][0]]
                            dve.wait_ge(pv_done, 1 + it * H + 4 * g + 4)
                            dve.wait_ge(rinv_T_ready, it * G + g + 1)
                            dve.wait_ge(ctx_split, 1 + it * G + g)
                            dve.scalar_tensor_tensor(out=ctx32[:, :], in0=bank[:, :], scalar=1.0 / PS,
                                                     in1=rinv_T[:, :], op0=ALU.mult, op1=ALU.mult)\
                                .then_inc(ctx_ready, 1)
                        if n == ctx_slot(g) + 1:
                            dve.wait_ge(ctx_hi, it * G + g + 1)
                            dve.wait_ge(ctx_ready, 1 + it * G + g + 1)
                            dve.scalar_tensor_tensor(out=xT[1][:, g, :], in0=ctx32[:, :], scalar=bv[:, g:g + 1],
                                                     in1=xT[0][:, g, :], op0=ALU.add, op1=ALU.subtract)\
                                .then_inc(ctx_split, 1)
                    if n < HT:
                        h, j = n // T, n % T
                        half = n // 2
                        bank = arrived(dve, it, ("S", h, j))
                        if j % 2 == 0:
                            dve.wait_ge(bias_in[half % NB], (it * (2 * H // NB) + half // NB + 1) * 16)
                        dve.wait_ge(prob_ready, 1 + it * HT + max(0, n - NT + 1))
                        dve.sem_inc(carrier, 1)
                        dve.tensor_tensor_reduce(negs[:, j % NT, :], bank[:, :], bias[:, half % NB, j % 2, :],
                                                 -1.0, 3.0e38, ALU.add, ALU.min, nmax[:, h % 2, j:j + 1])\
                            .then_inc(scored, 1)
                    if n in DVE_L0:
                        l0_part(link, it, DVE_L0[n])
                    if 0 <= n - LAG_T < HT:
                        h, j = (n - LAG_T) // T, (n - LAG_T) % T
                        lo_of(("T", h, j), n - LAG_T, pT[0][:, h % 2, j, :], pT[1][:, h % 2, j, :], pT_split, PS)
                for c in range(C):
                    l0_part(link, it, ("x1T", c))
                for t in range(T):
                    bank = arrived(dve, it, ("wo", t))
                    dve.wait_ge(x1b_ready, it * T + t + 1)
                    dve.scalar_tensor_tensor(out=x1[:, t, :], in0=bank[:, :], scalar=1.0 / WS, in1=x1[:, t, :],
                                             op0=ALU.mult, op1=ALU.add).then_inc(x2_ready, 1)
            assert links[0] == LINKS_A, [0, links[0]]


STEPS = 2 * NF
LAG_DOWN = 2
NW = 6
ALPHA = [3, 5, 7, 9]
STENCIL = {12: 0, 13: 1}
BETA = [11, 13, 15, 16]
SUM = [13, 14, NF, 17]
RELU = [14, 15, NF, 18]
CHUNK = {k: (4 + 2 * k if k < NW else NF + k - 3) for k in range(NF)}
NORM2 = 2 * NF - 9


def ffn_pass(nc, a, x2_dram, out):
    order, ring = [], 0

    def in_ring(key):
        nonlocal ring
        order.append((key, 4 + ring % 4))
        ring += 1

    for n in range(STEPS):
        if n == NF:
            order += [(("x3T", c), c) for c in range(C)]
            in_ring(("L3", 2))
            in_ring(("L3", 3))
        in_ring(("up", n))
        if n in STENCIL:
            in_ring(("L3", STENCIL[n]))
    for c in range(C):
        in_ring(("h2T", c))
    banks = Banks(order)

    with ExitStack() as ctx:
        def sb(name, shape, dt):
            return ctx.enter_context(nc.sbuf_tensor(name, shape, dt))

        def sem(name):
            return ctx.enter_context(nc.semaphore(name))

        w1 = [sb(f"w1_{h}", [P, C, FF], F16) for h in ("hi", "lo")]
        w2 = [sb(f"w2_{h}", [P, NF, D], F16) for h in ("hi", "lo")]
        wl = [sb(f"wl_{h}", [P, NW, 2 * D], F16) for h in ("hi", "lo")]
        raw = sb("raw2", [P, 2, 2 * D], F32)
        ident = sb("ident2", [P, P], F32)
        dmat = sb("dmat", [P, 10, P], F16)
        b1 = sb("b1", [P, NF], F32)
        bi = sb("bi", [P, NF], F32)
        dt = sb("dt", [P, B], F32)
        idx = sb("idx", [1, B], I32)
        g2, beta2, b2 = (sb(n, [P, D], F32) for n in ("g2", "beta2", "b2"))
        l2_rows = sb("l2_rows", [P, 3, D], F32)
        x2n = sb("x2n", [P, T, D], F32)
        x2 = sb("x2", [P, T, D], F32)
        h2 = sb("h2", [P, T, D], F32)
        f = sb("f", [P, T, D], F32)
        xT = [sb(f"x3T_{h}", [P, C, S], F16) for h in ("hi", "lo")]
        g32 = sb("g32", [P, 2, S], F32)
        gT = [sb(f"g2T_{h}", [P, 4, S], F16) for h in ("hi", "lo")]
        grid = sb("grid", [P, 3, D], F32)
        prod = sb("prod", [P, 4, D], F32)
        tmp = sb("tmp", [P, 2, D], F32)
        halo_w = sb("halo_w", [8, P], F16)
        halo = sb("halo", [8, T, D], F16)
        vsp = [sb(f"vsp_{h}", [P, T, D], F16) for h in ("hi", "lo")]
        msp = [sb(f"msp_{h}", [P, T, D], F16) for h in ("hi", "lo")]
        outt = sb("outt", [P, 2, D], F32)
        edge = sb("edge", [P, 4], F32)
        stats = sb("stats2", [P, T, 6], F32)
        mv = sb("mv2", [P, T, 2], F32)
        var = sb("var2", [P, T], F32)
        rstd = sb("rstd2", [P, T], F32)
        newt = sb("newt2", [P, T], F32)

        psum = [ctx.enter_context(nc.psum_tensor(f"ffn_bank{i}", [P, S], F32)) for i in range(8)]
        full = [sem(f"ffn_bank{i}_full") for i in range(8)]

        vec_in = sem("ffn_vec_in")
        idx_in = sem("idx_in")
        idx_clipped = sem("idx_clipped")
        dmat_in = sem("dmat_in")
        halo_in = sem("halo_in")
        w_raw_in = [sem(f"w_raw{i}_in") for i in range(6)]
        w_hi = sem("w_hi")
        w_split = sem("w_split")
        ident_set = sem("ffn_ident_set")
        zeroed = sem("zeroed")
        x2_in = sem("x2_in")
        rows_in = sem("rows_in")
        chunk_in = [sem(f"chunk{i}_in") for i in range(2)]
        chunk_hi = sem("chunk_hi")
        chunk_split = sem("chunk_split")
        alpha_in = sem("alpha_grids_in")
        beta_in = sem("beta_grids_in")
        hi_done = sem("ffn_hi_done")
        first_full = sem("first_h2T_full")
        h2T_split = sem("h2T_split")
        x3T_split = sem("x3T_split")
        gelu_ready = sem("gelu_ready")
        g_split = sem("ffn_g_split")
        down_done = sem("down_done")
        acc_full = sem("acc_full")
        x3_ready = sem("x3_ready")
        x3b_ready = sem("x3b_ready")
        r_ready = sem("r_ready")
        x2b_ready = sem("x2b_ready")
        scaled2 = sem("scaled2")
        h2_ready = sem("h2_ready")
        scaled3 = sem("scaled3")
        f_ready = sem("f_ready")
        alpha_prod = sem("alpha_prod")
        v_ready = sem("v_ready")
        grid_hi = sem("grid_hi")
        alpha_done = sem("alpha_done")
        beta_prod = sem("beta_prod")
        y_done = sem("y_part_done")
        sum_ready = sem("stencil_sum_ready")
        step_ready = sem("step_ready")
        out_ready = sem("out_ready")
        out_stored = [sem(f"out{i}_stored") for i in range(2)]
        chain = sem("ffn_dve_chain")
        carrier = sem("ffn_wait_carrier")

        block = ctx.enter_context(nc.Block())

        BEGUN = {"vector": (sum_ready, chunk_split, y_done, r_ready, g_split),
                 "gpsimd": (beta_prod,), "scalar": (gelu_ready, out_ready, *out_stored)}
        base = {s: 1 for sems in BEGUN.values() for s in sems}
        base[h2T_split] = C

        def begin(eng, name):
            for s in BEGUN[name]:
                eng.sem_inc(s, 1)

        def claim(pe, it, key):
            bank, _, last = banks.place[key]
            k = last[1]
            signal, per = {"h2T": (h2T_split, C), "x3T": (x3T_split, C), "up": (gelu_ready, STEPS),
                           "L3": (sum_ready, T)}[last[0]]
            pe.wait_ge(signal, base.get(signal, 0) + it * per + (0 if banks.first[key] else k + 1))
            return psum[bank]

        def arrived(eng, it, key):
            bank, before, _ = banks.place[key]
            eng.wait_ge(full[bank], it * banks.uses[bank] + before + 1)
            return psum[bank]

        def full_of(key):
            return full[banks.place[key][0]]

        def downs(n):
            return n + 1 - n // NF

        COLS = [(b1[:, :], a["b1"]), (dt[:, :], a["dt"].partition_broadcast(P)),
                (g2[:, :], a["g2"].partition_broadcast(P)), (beta2[:, :], a["beta2"].partition_broadcast(P)),
                (b2[:, :], a["b2"].partition_broadcast(P))]
        PIECES = []
        for c in range(C):
            for half in range(2):
                cols = slice(half * 1024, (half + 1) * 1024)
                PIECES.append((a["W1"][c * P:(c + 1) * P, cols], w1[0][:, c, cols], w1[1][:, c, cols]))
        for k in range(0, NF, 2):
            src = a["W2"][k * P:(k + 2) * P, :].rearrange("(k p) n -> p k n", p=P)
            PIECES.append((src, w2[0][:, k:k + 2, :], w2[1][:, k:k + 2, :]))

        RAWS = [raw[:, 0, :], raw[:, 1, :]]
        RAWS += [v.rearrange("p k d -> p (k d)") for v in (prod[:, 0:2, :], prod[:, 2:4, :], tmp[:, :, :], outt[:, :, :])]
        NR = len(RAWS)

        def piece_raw(i):
            v = RAWS[i % NR]
            return v if i < 2 * C else v.rearrange("p (k n) -> p k n", k=2)

        def after_loop(it):
            return isinstance(it, int)

        def stencil_load(sp, it, kind, t):
            rows = slice(t * P, (t + 1) * P)
            if kind == "alpha":
                if t:
                    sp.wait_ge(alpha_prod, it * 12 + 3 * t)
                else:
                    sp.wait_ge(beta_prod, 1 + it * 16)
                for i, g in enumerate((0, 2, 4)):
                    sp.dma_start(grid[:, i, :], a["grids"][g, rows, :]).then_inc(alpha_in, 16)
            else:
                into = grid
                if t:
                    sp.wait_ge(beta_prod, 1 + it * 16 + 4 * t)
                elif not after_loop(it):
                    sp.wait_ge(alpha_prod, it * 12 + 12)
                if after_loop(it):
                    into = x2n
                for i, g in enumerate((1, 3)):
                    sp.dma_start(into[:, i, :], a["grids"][g, rows, :]).then_inc(beta_in, 16)

        @block.sync
        def _(sp):
            sp.dma_start(idx[:, :], a["idx2"].rearrange("(o b) -> o b", o=1)).then_inc(idx_in, 16)
            sp.dma_start(x2n[:, :, :], x2_dram[0].rearrange("(t p) d -> p t d", p=P)).then_inc(x2_in, 16)
            for dst, src in COLS:
                sp.dma_start(dst, src).then_inc(vec_in, 16)
            sp.dma_start(dmat[:, :, :], a["dmat"]).then_inc(dmat_in, 16)
            sp.dma_start(halo_w[:, :], a["halo"]).then_inc(dmat_in, 16)
            for i, (src, _, _) in enumerate(PIECES):
                if i >= NR:
                    sp.wait_ge(w_split, i - NR + 1)
                sp.dma_start(piece_raw(i), src).then_inc(w_raw_in[i % NR], 16)
            sp.wait_ge(w_split, len(PIECES))
            sp.wait_ge(idx_clipped, 1)
            with sp.Fori(0, B) as it:
                e = sp.value_load(idx[0:1, bass.ds(it, 1)], min_val=0, max_val=NE2 - 1)

                def load_chunk(k):
                    sp.wait_ge(chunk_split, 1 + it * NF + max(0, k - 1))
                    sp.dma_start(raw[:, k % 2, :], a["W_l2"][e, k]).then_inc(chunk_in[k % 2], 16)

                def load_rows():
                    sp.wait_ge(f_ready, it * T + T)
                    sp.dma_start(bi[:, :], a["bi"][e]).then_inc(rows_in, 16)
                    sp.dma_start(l2_rows[:, :, :], a["rows2"][e].partition_broadcast(P)).then_inc(rows_in, 16)

                def load_next_x2():
                    sp.wait_ge(x2b_ready, it * T + T)
                    nxt = (it + 1) % B
                    sp.dma_start(x2n[:, :, :], x2_dram[nxt].rearrange("(t p) d -> p t d", p=P)).then_inc(x2_in, 16)

                def load_halo():
                    sp.wait_ge(alpha_done, it * T + T)
                    sp.wait_ge(zeroed, 3)
                    for k, part in enumerate((*vsp, *msp)):
                        sp.dma_start(halo[k:k + 1, 1:T, :], part[P - 1:P, 0:T - 1, :]).then_inc(halo_in, 16)
                        sp.dma_start(halo[4 + k:5 + k, 0:T - 1, :], part[0:1, 1:T, :]).then_inc(halo_in, 16)

                loads = [(CHUNK[k - 2] if k >= 2 else -1, 0, load_chunk, (k,)) for k in range(NF)]
                loads += [(ALPHA[t - 1] if t else -1, 1, stencil_load, (sp, it, "alpha", t)) for t in range(T)]
                loads += [(BETA[t - 1] if t else ALPHA[-1], 1, stencil_load, (sp, it, "beta", t)) for t in range(T)]
                loads += [(1, 2, load_rows, ()), (1, 3, load_next_x2, ()), (ALPHA[-1], 0, load_halo, ())]
                for _, _, load, args in sorted(loads, key=lambda x: x[:2]):
                    load(*args)
            sp.wait_ge(h2_ready, B * T + T)
            sp.wait_ge(x2b_ready, B * T + T)
            for t in range(T):
                stencil_load(sp, B, "alpha", t)
                stencil_load(sp, B, "beta", t)

        def add_beta3(pool, it):
            for t in range(T):
                pool.wait_ge(scaled3, it * T + t + 1)
                pool.tensor_tensor(f[:, t, :], f[:, t, :], l2_rows[:, 2, :], ALU.add).then_inc(f_ready, 1)

        def alpha_products(pool, it, t):
            pool.wait_ge(f_ready, it * T + t + 1)
            pool.wait_ge(alpha_in, (it * T + t + 1) * 48)
            if t:
                pool.wait_ge(alpha_done, it * T + t)
            else:
                pool.wait_ge(sum_ready, 1 + it * T)
            for i in (2, 0, 1):
                pool.tensor_tensor(prod[:, i, :], grid[:, i, :], f[:, t, :], ALU.mult).then_inc(alpha_prod, 1)

        def beta_products(pool, it, t):
            pool.wait_ge(beta_in, (it * T + t + 1) * 32)
            into, grids = (h2, x2n) if after_loop(it) else (prod, grid)
            if after_loop(it):
                pool.wait_ge(h2T_split, C + B * C)
            else:
                pool.wait_ge(alpha_done, it * T + T)
            pool.wait_ge(y_done, 1 + it * T + t)
            for i in range(2):
                pool.tensor_tensor(into[:, i, :], grids[:, i, :], f[:, t, :], ALU.mult).then_inc(beta_prod, 1)
            pool.wait_ge(beta_prod, 1 + it * 16 + 4 * t + 2)
            pool.tensor_tensor(into[:, 2, :], into[:, 1, :], into[:, 0, :], ALU.subtract).then_inc(beta_prod, 1)
            pool.tensor_tensor(into[:, 3, :], into[:, 1, :], into[:, 0, :], ALU.add).then_inc(beta_prod, 1)

        def move_x2(pool, t):
            pool.tensor_tensor(x2[:, t, :], x2n[:, t, :], b2[:, :], ALU.add).then_inc(x2b_ready, 1)

        @block.gpsimd
        def _(pool):
            begin(pool, "gpsimd")
            pool.memset(ident[:, :], 0.0).then_inc(ident_set, 1)
            pool.wait_ge(ident_set, 1)
            pool.affine_select(out=ident[:, :], in_=ident[:, :], compare_op=ALU.not_equal, fill=1.0, base=0,
                               pattern=[[-1, P]], channel_multiplier=1).then_inc(ident_set, 1)
            pool.memset(f[:, :, :], 0.0).then_inc(zeroed, 1)
            pool.memset(l2_rows[:, :, :], 0.0).then_inc(zeroed, 1)
            pool.memset(halo[:, :, :].rearrange("p t d -> p (t d)").bitcast(F32), 0.0).then_inc(zeroed, 1)
            pool.wait_ge(vec_in, 16 * len(COLS))
            pool.wait_ge(x2_in, 16)
            pool.wait_ge(zeroed, 2)
            for t in range(T):
                move_x2(pool, t)
            for t in range(T):
                pool.wait_ge(scaled2, t + 1)
                pool.tensor_tensor(h2[:, t, :], h2[:, t, :], beta2[:, :], ALU.add).then_inc(h2_ready, 1)
            with pool.Fori(0, B) as it:
                add_beta3(pool, it)
                for t in range(T):
                    alpha_products(pool, it, t)
                for t in range(T):
                    beta_products(pool, it, t)
                arrived(pool, it, ("x3T", C - 1))
                pool.wait_ge(rows_in, it * 32 + 32)
                for t in range(T):
                    pool.tensor_tensor(x2[:, t, :], x2[:, t, :], l2_rows[:, 0, :], ALU.add).then_inc(x3b_ready, 1)
                for t in range(T):
                    pool.wait_ge(scaled2, it * T + T + t + 1)
                    pool.tensor_tensor(h2[:, t, :], h2[:, t, :], beta2[:, :], ALU.add).then_inc(h2_ready, 1)
                for t in range(T):
                    pool.wait_ge(r_ready, 1 + it * T + t + 1)
                    move_x2(pool, t)
            add_beta3(pool, B)
            for t in range(T):
                alpha_products(pool, B, t)
                beta_products(pool, B, t)

        def stencil(pe, bank, t, rows_beside):
            terms = []
            for m, parts in ((0, vsp), (5, msp)):
                diag = m + (0 if t == 0 else 2 if t == T - 1 else 1)
                for blk, tt in ((diag, t), (m + 3, t - 1), (m + 4, t + 1)):
                    if 0 <= tt < T and not (rows_beside and tt != t):
                        terms += [(dmat[:, blk, :], part[:, tt, :]) for part in parts]
            if rows_beside:
                terms.append((halo_w[:, :], halo[:, t, :]))
            for i, (w, x) in enumerate(terms):
                mm = pe.matmul(bank[:, :], w, x, start=(i == 0), stop=(i == len(terms) - 1))
            return mm

        @block.tensor
        def _(pe):
            def three(out, w, x, first, last):
                pe.matmul(out, w[0], x[0], start=first, stop=False)
                pe.matmul(out, w[0], x[1], start=False, stop=False)
                return pe.matmul(out, w[1], x[0], start=False, stop=last)

            pe.wait_ge(ident_set, 2)
            pe.wait_ge(w_split, 2 * C)
            pe.wait_ge(dmat_in, 32)
            def h2_transposes(bank, c):
                for t in range(T):
                    mm = pe.transpose(bank[:, t * P:(t + 1) * P], h2[:, t, c * P:(c + 1) * P], ident[:, :])
                return mm

            pe.wait_ge(h2_ready, T)
            for c in range(C):
                h2_transposes(psum[c], c).then_inc(first_full, 1)
            with pe.Fori(0, B) as it:
                def up(n):
                    bank = claim(pe, it, ("up", n))
                    k = n % NF
                    if n >= NF:
                        pe.wait_ge(chunk_split, 1 + it * NF + k + 1)
                    for c in range(C):
                        if n % NF == 0:
                            if n:
                                pe.wait_ge(x3T_split, it * C + c + 1)
                            else:
                                pe.wait_ge(h2T_split, it * C + C)
                        w = [x[:, c, k * P:(k + 1) * P] for x in w1] if n < NF else \
                            [x[:, k % NW, c * P:(c + 1) * P] for x in wl]
                        mm = three(bank[:, :], w, [x[:, c, :] for x in xT], c == 0, c == C - 1)
                    mm.then_inc(full_of(("up", n)), 1)

                def down(n):
                    k = n % NF
                    if n == 0:
                        pe.wait_ge(w_split, len(PIECES))
                    pe.wait_ge(g_split, 1 + it * STEPS + n + 1)
                    w = [x[:, k, :] for x in w2] if n < NF else [x[:, k % NW, D:2 * D] for x in wl]
                    for t in range(T):
                        if n == 0 and t == 0:
                            pe.wait_ge(r_ready, 1 + it * T)
                        mm = three(psum[t][:, :], [x[:, n % 4, t * P:(t + 1) * P] for x in gT], w, k == 0, k == NF - 1)
                        if k == NF - 1:
                            mm.then_inc(acc_full, 1)
                    if k < NF - 1:
                        mm.then_inc(down_done, 1)

                def run_stencil(t):
                    bank = claim(pe, it, ("L3", t))
                    pe.wait_ge(alpha_done, it * T + T)
                    pe.wait_ge(halo_in, it * 128 + 128)
                    stencil(pe, bank, t, True).then_inc(full_of(("L3", t)), 1)

                for half in range(2):
                    if half:
                        run_stencil(2)
                        for t in range(T):
                            pe.wait_ge(x3_ready, it * T + T)
                            for c in range(C):
                                mm = pe.transpose(psum[c][:, t * P:(t + 1) * P], x2[:, t, c * P:(c + 1) * P], ident[:, :])
                                if t == T - 1:
                                    mm.then_inc(full_of(("x3T", c)), 1)
                        run_stencil(3)
                    for n in range(half * NF, half * NF + NF):
                        up(n)
                        if n - LAG_DOWN >= half * NF:
                            down(n - LAG_DOWN)
                        if n in STENCIL:
                            run_stencil(STENCIL[n])
                    if half:
                        pe.wait_ge(h2_ready, it * T + 2 * T)
                        for c in range(C):
                            h2_transposes(claim(pe, it, ("h2T", c)), c).then_inc(full_of(("h2T", c)), 1)
                    for n in range(half * NF + NF - LAG_DOWN, half * NF + NF):
                        down(n)
            pe.wait_ge(r_ready, 1 + B * T)
            for t in range(T):
                pe.wait_ge(alpha_done, B * T + min(T, t + 2))
                stencil(pe, psum[t], t, False).then_inc(full[t], 1)

        def relu_store(act, it, row, t):
            act.wait_ge(step_ready, it * T + t + 1)
            act.wait_ge(out_stored[t % 2], 1 + (it * (T // 2) + t // 2) * 16)
            act.activation(outt[:, t % 2, :], tmp[:, 1, :], ACT.Relu).then_inc(out_ready, 1)
            act.wait_ge(out_ready, 1 + it * T + t + 1)
            act.dma_start(out[row, t * P:(t + 1) * P, :], outt[:, t % 2, :]).then_inc(out_stored[t % 2], 16)

        def alpha_hi(act, it, t):
            act.wait_ge(alpha_prod, it * 12 + 3 * t + 3)
            act.activation(msp[0][:, t, :], prod[:, 1, :], ACT.Copy).then_inc(grid_hi, 1)
            act.wait_ge(v_ready, it * T + t + 1)
            act.activation(vsp[0][:, t, :], tmp[:, 0, :], ACT.Copy).then_inc(grid_hi, 1)

        @block.scalar
        def _(act):
            begin(act, "scalar")
            act.wait_ge(vec_in, 16 * len(COLS))
            for i, (_, hi, _) in enumerate(PIECES):
                if i == 2 * C:
                    for c in range(C):
                        act.wait_ge(first_full, c + 1)
                        act.activation(xT[0][:, c, :], psum[c][:, :], ACT.Copy).then_inc(hi_done, 1)
                act.wait_ge(w_raw_in[i % NR], 16 * (i // NR + 1))
                act.activation(hi, piece_raw(i), ACT.Copy, scale=WS).then_inc(w_hi, 1)
            with act.Fori(0, B) as it:
                prev = (it + (B - 1)) % B

                def copy_hi(key, c):
                    bank = arrived(act, it, key)
                    act.activation(xT[0][:, c, :], bank[:, :], ACT.Copy).then_inc(hi_done, 1)

                for n in range(STEPS):
                    if n == NF:
                        for c in range(C):
                            copy_hi(("x3T", c), c)
                        act.wait_ge(rows_in, it * 32 + 32)
                    bank = arrived(act, it, ("up", n))
                    act.wait_ge(g_split, 1 + it * STEPS + max(0, n - 1))
                    func, vec = (ACT.Gelu_apprx_sigmoid, b1) if n < NF else (ACT.Gelu, bi)
                    act.activation(g32[:, n % 2, :], bank[:, :], func, scale=1.0 / WS,
                                   bias=vec[:, n % NF:n % NF + 1]).then_inc(gelu_ready, 1)
                    for k in range(NF):
                        if CHUNK[k] == n:
                            act.wait_ge(chunk_in[k % 2], (it * (NF // 2) + k // 2 + 1) * 16)
                            if k >= NW:
                                act.wait_ge(down_done, it * (STEPS - 2) + downs(NF + k - NW))
                            act.activation(wl[0][:, k % NW, :], raw[:, k % 2, :], ACT.Copy, scale=WS)\
                                .then_inc(chunk_hi, 1)
                    if n in ALPHA:
                        alpha_hi(act, it, ALPHA.index(n))
                    if n in RELU:
                        relu_store(act, it, prev, RELU.index(n))
                for c in range(C):
                    copy_hi(("h2T", c), c)
            for t in range(T + 1):
                if t < T:
                    alpha_hi(act, B, t)
                if t:
                    relu_store(act, B, B - 1, t - 1)
            for stored in out_stored:
                act.wait_ge(stored, 1 + (B + 1) * (T // 2) * 16)

        @block.vector
        def _(dve):
            links = [0]

            def mark(ins):
                links[0] += 1
                return ins.then_inc(chain, 1)

            def chained(base):
                def link(ins):
                    mark(ins)
                    dve.wait_ge(chain, base + links[0])
                return link

            def norm_stats(link, src, tiles):
                for t in tiles[:-1]:
                    mark(dve.bn_stats(stats[:, t, :], src[:, t, :]))
                link(dve.bn_stats(stats[:, tiles[-1], :], src[:, tiles[-1], :]))
                dve.sem_inc(carrier, 1)
                for t in tiles[:-1]:
                    mark(dve.bn_aggr(mv[:, t, :], stats[:, t, :]))
                link(dve.bn_aggr(mv[:, tiles[-1], :], stats[:, tiles[-1], :]))

            def norm_rstd(link, eps):
                link(dve.tensor_scalar(var[:, :], mv[:, :, 1], eps, None, ALU.add))
                rsqrt_steps(dve, link, var[:, :], rstd[:, :], newt[:, :], rstd[:, :].bitcast(I32),
                            var[:, :].bitcast(I32))

            def norm_scale(link, dst, src, gain, tiles, signal):
                for t in tiles:
                    step = link if t == tiles[-1] else mark
                    step(dve.tensor_scalar(dst[:, t, :], src[:, t, :], mv[:, t, 0:1], rstd[:, t:t + 1],
                                           ALU.subtract, ALU.mult))
                for t in tiles:
                    dve.tensor_tensor(dst[:, t, :], dst[:, t, :], gain, ALU.mult).then_inc(signal, 1)

            def norm3(link, it, part):
                if part == 0:
                    norm_stats(link, f, range(T))
                else:
                    if part == 1:
                        norm_rstd(link, 1e-12)
                    norm_scale(link, f, f, l2_rows[:, 1, :], (2 * part - 2, 2 * part - 1), scaled3)

            def alpha(link, it, t):
                dve.wait_ge(alpha_prod, it * 12 + 3 * t + 3)
                m0, m2, m1 = prod[:, 0, :], prod[:, 1, :], prod[:, 2, :]
                w = tmp[:, 0, :]
                mark(dve.tensor_tensor(w[:, 1:D - 1], m1[:, 2:D], m1[:, 0:D - 2], ALU.subtract))
                ends = [m1[:, k:D - k:D - 1 - 2 * k] for k in range(3)]
                we = w[:, 0:D:D - 1]
                link(dve.tensor_scalar(we, ends[0], -3.0, None, ALU.mult))
                link(dve.scalar_tensor_tensor(out=we, in0=ends[1], scalar=4.0, in1=we, op0=ALU.mult, op1=ALU.add))
                link(dve.scalar_tensor_tensor(out=we, in0=ends[2], scalar=-1.0, in1=we, op0=ALU.mult, op1=ALU.add))
                link(dve.tensor_scalar(w[:, D - 1:D], w[:, D - 1:D], -1.0, None, ALU.mult))
                dve.scalar_tensor_tensor(out=w, in0=w, scalar=0.5, in1=m0, op0=ALU.mult, op1=ALU.subtract)\
                    .then_inc(v_ready, 1)
                dve.wait_ge(grid_hi, it * 2 * T + 2 * t + 1)
                dve.tensor_tensor(msp[1][:, t, :], m2, msp[0][:, t, :], ALU.subtract)
                dve.wait_ge(grid_hi, it * 2 * T + 2 * t + 2)
                dve.tensor_tensor(vsp[1][:, t, :], w, vsp[0][:, t, :], ALU.subtract).then_inc(alpha_done, 1)

            def y_part(it, t):
                return x2[:, t, :] if after_loop(it) else tmp[:, 0, :]

            def beta(link, it, t):
                dve.wait_ge(beta_prod, 1 + it * 16 + 4 * t + 4)
                dve.wait_ge(alpha_done, it * T + (t + 1 if after_loop(it) else T))
                pa, pb, less, plus = ((h2 if after_loop(it) else prod)[:, i, :] for i in range(4))
                s = y_part(it, t)
                ea = [pa[:, k:D - k:D - 1 - 2 * k] for k in range(3)]
                eb = [pb[:, k:D - k:D - 1 - 2 * k] for k in range(4)]
                sa, sbb = edge[:, 0:2], edge[:, 2:4]
                mark(dve.tensor_tensor(s[:, 1:D - 1], less[:, 2:D], plus[:, 0:D - 2], ALU.add))
                mark(dve.tensor_scalar(sa, ea[0], 1.5, None, ALU.mult))
                link(dve.scalar_tensor_tensor(out=sbb, in0=eb[1], scalar=-2.5, in1=eb[0], op0=ALU.mult, op1=ALU.add))
                mark(dve.scalar_tensor_tensor(out=s[:, 1:D - 1], in0=s[:, 1:D - 1], scalar=0.5, in1=pb[:, 1:D - 1],
                                              op0=ALU.mult, op1=ALU.subtract))
                mark(dve.scalar_tensor_tensor(out=sa, in0=ea[1], scalar=-2.0, in1=sa, op0=ALU.mult, op1=ALU.add))
                link(dve.scalar_tensor_tensor(out=sbb, in0=eb[2], scalar=2.0, in1=sbb, op0=ALU.mult, op1=ALU.add))
                mark(dve.scalar_tensor_tensor(out=sa, in0=ea[2], scalar=0.5, in1=sa, op0=ALU.mult, op1=ALU.add))
                link(dve.scalar_tensor_tensor(out=sbb, in0=eb[3], scalar=-0.5, in1=sbb, op0=ALU.mult, op1=ALU.add))
                link(dve.tensor_tensor(s[:, 0:1], sbb[:, 0:1], sa[:, 0:1], ALU.add))
                dve.tensor_tensor(s[:, D - 1:D], sbb[:, 1:2], sa[:, 1:2], ALU.subtract).then_inc(y_done, 1)

            def total(it, row, t, bank):
                s = y_part(it, t)
                dve.wait_ge(y_done, 1 + it * T + t + 1)
                if bank is None:
                    bank = arrived(dve, it, ("L3", t))
                else:
                    dve.wait_ge(full[t], B + 1)
                dve.wait_ge(out_ready, 1 + it * T + t)
                dve.tensor_tensor(tmp[:, 1, :], bank[:, :], s, ALU.add).then_inc(sum_ready, 1)
                dve.wait_ge(sum_ready, 1 + it * T + t + 1)
                dve.scalar_tensor_tensor(out=tmp[:, 1, :], in0=tmp[:, 1, :], scalar=row, in1=f[:, t, :],
                                         op0=ALU.mult, op1=ALU.add).then_inc(step_ready, 1)

            begin(dve, "vector")
            link = chained(0)
            dve.wait_ge(idx_in, 16)
            dve.tensor_scalar(idx[:, :], idx[:, :], 0, NE2 - 1, ALU.max, ALU.min).then_inc(idx_clipped, 1)
            dve.wait_ge(x2_in, 16)
            dve.wait_ge(vec_in, 16 * len(COLS))
            dve.wait_ge(zeroed, 2)
            norm_stats(link, x2n, range(T))
            norm_rstd(link, 1e-5)
            norm_scale(link, h2, x2n, g2[:, :], range(T), scaled2)
            for i, (_, hi, lo) in enumerate(PIECES):
                if i == 2 * C:
                    for c in range(C):
                        dve.wait_ge(hi_done, c + 1)
                        dve.tensor_tensor(xT[1][:, c, :], psum[c][:, :], xT[0][:, c, :], ALU.subtract)\
                            .then_inc(h2T_split, 1)
                dve.wait_ge(w_hi, i + 1)
                dve.scalar_tensor_tensor(out=lo, in0=piece_raw(i), scalar=WS, in1=hi,
                                         op0=ALU.mult, op1=ALU.subtract).then_inc(w_split, 1)
            before = links[0]

            with dve.Fori(0, B) as it:
                links[0] = 0
                link = chained(it * LINKS_B + before)
                prev = (it + (B - 1)) % B

                def lo_of(key, k, c, signal):
                    dve.wait_ge(hi_done, C + it * 2 * C + k + 1)
                    dve.tensor_tensor(xT[1][:, c, :], psum[banks.place[key][0]][:, :], xT[0][:, c, :], ALU.subtract)\
                        .then_inc(signal, 1)

                for n in range(STEPS):
                    if n == NF:
                        for t in range(T):
                            dve.wait_ge(acc_full, it * 2 * T + t + 1)
                            dve.wait_ge(x2b_ready, it * T + t + 1)
                            dve.scalar_tensor_tensor(out=x2[:, t, :], in0=psum[t][:, :], scalar=1.0 / WS,
                                                     in1=x2[:, t, :], op0=ALU.mult, op1=ALU.add).then_inc(x3_ready, 1)
                        for c in range(C):
                            lo_of(("x3T", c), c, c, x3T_split)
                        total(it, dt[:, bass.ds(prev, 1)], 2, None)
                    dve.wait_ge(gelu_ready, 1 + it * STEPS + n + 1)
                    if n >= 4 and (n - 4) % NF != NF - 1:
                        dve.wait_ge(down_done, it * (STEPS - 2) + downs(n - 4))
                    link(dve.tensor_copy(gT[0][:, n % 4, :], g32[:, n % 2, :]))
                    dve.tensor_tensor(gT[1][:, n % 4, :], g32[:, n % 2, :], gT[0][:, n % 4, :], ALU.subtract)\
                        .then_inc(g_split, 1)
                    for k in range(NF):
                        if CHUNK[k] == n:
                            dve.wait_ge(chunk_hi, it * NF + k + 1)
                            dve.scalar_tensor_tensor(out=wl[1][:, k % NW, :], in0=raw[:, k % 2, :], scalar=WS,
                                                     in1=wl[0][:, k % NW, :], op0=ALU.mult, op1=ALU.subtract)\
                                .then_inc(chunk_split, 1)
                    if n < 3:
                        norm3(link, it, n)
                    if n in ALPHA:
                        alpha(link, it, ALPHA.index(n))
                    if n in SUM and n != NF:
                        total(it, dt[:, bass.ds(prev, 1)], SUM.index(n), None)
                    if n in BETA:
                        beta(link, it, BETA.index(n))
                    if n == NORM2:
                        dve.wait_ge(x2_in, it * 16 + 32)
                        norm_stats(link, x2n, range(T))
                    if n == NORM2 + 1:
                        norm_rstd(link, 1e-5)
                    if n in (NORM2 + 2, NORM2 + 3):
                        norm_scale(link, h2, x2n, g2[:, :], range(2 * (n - NORM2 - 2), 2 * (n - NORM2 - 1)), scaled2)
                for c in range(C):
                    lo_of(("h2T", c), C + c, c, h2T_split)
                for t in range(T):
                    dve.wait_ge(acc_full, it * 2 * T + T + t + 1)
                    dve.wait_ge(x3b_ready, it * T + t + 1)
                    dve.scalar_tensor_tensor(out=f[:, t, :], in0=psum[t][:, :], scalar=1.0 / WS, in1=x2[:, t, :],
                                             op0=ALU.mult, op1=ALU.add).then_inc(r_ready, 1)
                dve.wait_ge(r_ready, 1 + it * T + T)
            assert links[0] == LINKS_B, [1, links[0]]
            link = chained(B * LINKS_B + before)
            links[0] = 0
            for part in range(3):
                norm3(link, B, part)
            dve.wait_ge(x2b_ready, B * T + T)
            for t in range(T + 1):
                if t < T:
                    alpha(link, B, t)
                    beta(link, B, t)
                if t:
                    total(B, dt[:, B - 1:B], t - 1, psum[t - 1])


def four_layers(nc, a, out):
    ada_rows = nc.dram_tensor("ada_rows", (B, 2 * D), F32).ap()
    x2 = nc.dram_tensor("x2_rows", (B, S, D), F32).ap()
    attention_pass(nc, a, ada_rows, x2)
    ffn_pass(nc, a, x2, out)


def stencil_blocks():
    d1, d2 = np.zeros((S, S)), np.zeros((S, S))
    for i in range(1, S - 1):
        d1[i, i - 1:i + 2] = -0.5, 0, 0.5
        d2[i, i - 1:i + 2] = 0.5, -1, 0.5
    d1[0, :3] = -1.5, 2, -0.5
    d1[-1, -3:] = 0.5, -2, 1.5
    d2[0, :4] = 1, -2.5, 2, -0.5
    d2[-1, -4:] = -0.5, 2, -2.5, 1
    cut = [m[i * P:(i + 1) * P, j * P:(j + 1) * P].T
           for m in (d1, d2) for i, j in ((0, 0), (1, 1), (T - 1, T - 1), (1, 0), (1, 2))]
    return np.stack(cut, 1).astype(np.float16)


def halo_weights():
    w = np.zeros((8, P), np.float16)
    w[:, 0][:4] = -0.5, -0.5, 0.5, 0.5
    w[4:, P - 1] = 0.5
    return w


def laid_out(inputs):
    w = {n: np.ascontiguousarray(np.asarray(v)) for n, v in inputs.items()}
    col = lambda v: v.reshape(-1, P).T
    half = D // 2
    a = {
        "x": w["x"], "dom": w["itok_B_0_15"], "steps": w["itok_B_34_63"], "idx2": w["itok_B_0_7"],
        "dt": w["condB_dt"], "bias": w["fside_Bx16xSxS_0"], "mask": w["mask_Bx1xSxS_bk0"][:, 0],
        "freqs": col(np.exp(np.arange(half, dtype=np.float32) * np.float32(-math.log(10000.0) / (half - 1)))),
        "dmat": stencil_blocks(), "halo": halo_weights(),
        "exp_WT": w["L0_cond_expert_W"].transpose(0, 2, 1),
        "exp_vec": np.stack([w["L0_cond_expert_b"], w["L0_cond_domain_emb"]], -1),
        "down_WT": w["L0_cond_down_W"].T.reshape(C, P, A).transpose(1, 0, 2),
        "up_WT": w["L0_cond_up_W"].T,
        "down_b": col(w["L0_cond_down_b"]), "up_b": w["L0_cond_up_b"],
        "ln_g": w["L0_cond_ln_gamma"], "ln_b": w["L0_cond_ln_beta"],
        "W_l2": np.concatenate([
            w["L2_cond_Wi"].reshape(NE2, C, P, NF, P).transpose(0, 3, 2, 1, 4).reshape(NE2, NF, P, D),
            w["L2_cond_Wo"].reshape(NE2, NF, P, D)], -1),
        "bi": w["L2_cond_bi"].reshape(NE2, NF, P).transpose(0, 2, 1),
        "rows2": np.stack([w["L2_cond_bo"], w["L2_cond_gamma"], w["L2_cond_beta"]], 1),
        "grids": np.concatenate([w["L3_cond_A_grid"], w["L3_cond_B_grid"]], 0),
    }
    for n in ("W_ada", "b_ada", "Wq", "Wk", "Wv", "Wo", "bo", "W1", "W2", "b2", "g2", "beta2"):
        a[n] = w["L1_cond_" + n]
    for n in ("bq", "bk", "bv", "b1"):
        a[n] = col(w["L1_cond_" + n])
    return {n: np.ascontiguousarray(v) for n, v in a.items()}


def kernel(**inputs):
    import concourse.bacc as bacc
    from concourse.bass_utils import run_bass_kernel_spmd

    nc = bacc.Bacc("TRN2", target_bir_lowering=False, num_devices=1)
    arrays = {"in_" + n: v for n, v in laid_out(inputs).items()}
    a = {n[3:]: nc.dram_tensor(n, v.shape, mybir.dt.from_np(v.dtype), kind="ExternalInput").ap()
         for n, v in arrays.items()}
    out = nc.dram_tensor("out", (B, S, D), F32, kind="ExternalOutput").ap()
    four_layers(nc, a, out)
    return run_bass_kernel_spmd(nc, [arrays], core_ids=[0]).results[0]["out"]
```
